# Optimizing a Trainium2 kernel written in Bass

```python
import numpy as np
import jax
import jax.numpy as jnp

def _softmax(x, axis=-1):
    return jax.nn.softmax(x, axis=axis)

def _gelu(x):
    return jax.nn.gelu(x, approximate=True)

def _silu(x):
    return jax.nn.silu(x)

def _sigmoid(x):
    return jax.nn.sigmoid(x)

def _layernorm(x, axis=-1, eps=1e-05):
    m = jnp.mean(x, axis=axis, keepdims=True)
    v = jnp.var(x, axis=axis, keepdims=True)
    return (x - m) / jnp.sqrt(v + eps)

def _scatter_add(tgt, idx, src, axis=0):
    return tgt.at[idx].add(src)

def _segment_sum(src, seg, n):
    return jax.ops.segment_sum(src, seg, n)
kernel_name = 'mk_macaron_d1_jaxref_r8_1f7a91'

def setup_inputs(seed: int=0):
    np.random.seed(seed)
    _w = jnp.asarray

    def _L0_attn_setup():
        import jax, jax.numpy as jnp
        import numpy as np
        B, L, D = (2, 256, 128)
        K, M, A = (32, 4, 4)
        H = D // K
        CK = 4
        TOTAL = 2 * D + K

        def _glorot(k, shape):
            lim = np.sqrt(6.0 / (shape[0] + shape[1]))
            return jax.random.uniform(k, shape, jnp.float32, -lim, lim)
        key = jax.random.key(seed)
        ks = jax.random.split(key, 8)
        grid = np.linspace(-np.pi / 3, np.pi / 3, M, dtype=np.float32)
        theta = np.tile(grid.reshape(1, 1, 1, 1, M), (1, 1, K, H, 1)).astype(np.float32)
        dr = np.geomspace(0.001, 0.1, K - A).astype(np.float32)
        ar = np.geomspace(0.01, 0.1, A).astype(np.float32)
        return {'x': jax.random.normal(ks[0], (B, L, D), jnp.float32), 'in_proj_w': _glorot(ks[1], (D, TOTAL)), 'conv_w': jax.random.normal(ks[2], (CK, 1, TOTAL), jnp.float32) * 0.1, 'conv_b': jnp.zeros((TOTAL,), jnp.float32), 'theta': jnp.asarray(theta), 'decay_slopes': jnp.asarray(np.log(np.exp(dr) - 1.0)), 'anchor_slopes': jnp.asarray(np.log(np.exp(ar) - 1.0)), 'score_scale': jnp.ones((K,), jnp.float32), 'deriv_logits': jnp.asarray([5.0, 0.0, 0.0], jnp.float32), 'norm_scale': jnp.ones((2 * H * M,), jnp.float32), 'W_re': _glorot(ks[3], (H * M, H)), 'W_im': _glorot(ks[4], (H * M, H)), 'out_proj_w': _glorot(ks[5], (D, D))}
    _L0_attn_in = _L0_attn_setup()

    def _L0_ffn_setup():
        import jax, jax.numpy as jnp
        import numpy as np
        B, S, D, H, E = (4, 256, 128, 512, 8)
        key = jax.random.key(seed)
        ks = jax.random.split(key, 8)
        s_d = 1.0 / np.sqrt(D)
        s_h = 1.0 / np.sqrt(H)
        return {'x': jax.random.normal(ks[0], (B, S, D), dtype=jnp.float32), 'gate_w': jax.random.uniform(ks[1], (E, D), jnp.float32, -s_d, s_d), 'gate_b': jax.random.uniform(ks[2], (E,), jnp.float32, -s_d, s_d), 'w1': jax.random.uniform(ks[3], (E, H, D), jnp.float32, -s_d, s_d), 'b1': jax.random.uniform(ks[4], (E, H), jnp.float32, -s_d, s_d), 'w2': jax.random.uniform(ks[5], (E, D, H), jnp.float32, -s_h, s_h), 'b2': jax.random.uniform(ks[6], (E, D), jnp.float32, -s_h, s_h)}
    _L0_ffn_in = _L0_ffn_setup()
    _d = {'L0_attn_x': _L0_attn_in['x'], 'L0_attn_in_proj_w': _L0_attn_in['in_proj_w'], 'L0_attn_conv_w': _L0_attn_in['conv_w'], 'L0_attn_conv_b': _L0_attn_in['conv_b'], 'L0_attn_theta': _L0_attn_in['theta'], 'L0_attn_decay_slopes': _L0_attn_in['decay_slopes'], 'L0_attn_anchor_slopes': _L0_attn_in['anchor_slopes'], 'L0_attn_score_scale': _L0_attn_in['score_scale'], 'L0_attn_deriv_logits': _L0_attn_in['deriv_logits'], 'L0_attn_norm_scale': _L0_attn_in['norm_scale'], 'L0_attn_W_re': _L0_attn_in['W_re'], 'L0_attn_W_im': _L0_attn_in['W_im'], 'L0_attn_out_proj_w': _L0_attn_in['out_proj_w'], 'L0_ffn_gate_w': _L0_ffn_in['gate_w'], 'L0_ffn_gate_b': _L0_ffn_in['gate_b'], 'L0_ffn_w1': _L0_ffn_in['w1'], 'L0_ffn_b1': _L0_ffn_in['b1'], 'L0_ffn_w2': _L0_ffn_in['w2'], 'L0_ffn_b2': _L0_ffn_in['b2']}
    _x0 = _d['L0_attn_x']
    _d['L0_attn_x'] = jax.random.normal(jax.random.fold_in(jax.random.key(seed), 1), (1, 2048, 128), dtype=_x0.dtype)
    del _x0
    return _d

def reference(L0_attn_x, L0_attn_in_proj_w, L0_attn_conv_w, L0_attn_conv_b, L0_attn_theta, L0_attn_decay_slopes, L0_attn_anchor_slopes, L0_attn_score_scale, L0_attn_deriv_logits, L0_attn_norm_scale, L0_attn_W_re, L0_attn_W_im, L0_attn_out_proj_w, L0_ffn_gate_w, L0_ffn_gate_b, L0_ffn_w1, L0_ffn_b1, L0_ffn_w2, L0_ffn_b2):

    def _L0_attn_ref(x, in_proj_w, conv_w, conv_b, theta, decay_slopes, anchor_slopes, score_scale, deriv_logits, norm_scale, W_re, W_im, out_proj_w):
        import jax, jax.numpy as jnp
        import numpy as np
        B, L, D = (2, 256, 128)
        K, M, A = (32, 4, 4)
        H = D // K
        CK = 4
        TOTAL = 2 * D + K

        def _glorot(k, shape):
            lim = np.sqrt(6.0 / (shape[0] + shape[1]))
            return jax.random.uniform(k, shape, jnp.float32, -lim, lim)
        b, l, d = x.shape
        z = x @ in_proj_w
        zp = jnp.pad(z, ((0, 0), (CK - 1, 0), (0, 0)))
        z = jax.lax.conv_general_dilated(zp, conv_w, (1,), 'VALID', dimension_numbers=('NWC', 'WIO', 'NWC'), feature_group_count=TOTAL) + conv_b
        x_val = z[..., :D].reshape(b, l, K, H)
        x_gate = jax.nn.silu(z[..., D:2 * D])
        s_raw = z[..., -K:].reshape(b, l, K, 1)
        pos = jnp.arange(l, dtype=jnp.float32)
        d_slopes = jax.nn.softplus(decay_slopes).reshape(1, 1, K - A, 1)
        dist_d = jnp.maximum(jnp.float32(l - 1) - pos, 0.0)[None, :, None, None]
        w_decay = jnp.exp(-d_slopes * dist_d)
        a_slopes = jax.nn.softplus(anchor_slopes).reshape(1, 1, A, 1)
        w_anchor = jnp.exp(-a_slopes * pos[None, :, None, None])
        time_weight = jnp.concatenate([w_decay, w_anchor], axis=2)
        p = jnp.exp(jnp.clip(score_scale[None, None, :, None] * s_raw, -20.0, 20.0))
        x5 = x_val[..., None]
        phi = x5 * theta
        cos_b, sin_b = (jnp.cos(phi), jnp.sin(phi))
        w = jax.nn.softmax(deriv_logits)
        poly = w[0] + w[1] * x5 - w[2] * jnp.square(x5)
        re_m = poly * cos_b
        im_m = poly * sin_b
        p_w = (p * time_weight)[..., None]
        flat = (b, l, K * H * M)
        merged = jnp.concatenate([(p_w * re_m).reshape(flat), (p_w * im_m).reshape(flat), jnp.broadcast_to(p_w, (b, l, K, H, M)).reshape(flat)], axis=-1)
        num_re, num_im, den = jnp.split(jnp.cumsum(merged, axis=1), 3, axis=-1)
        inv_den = 1.0 / jnp.maximum(den, jnp.float32(0.0001))
        re = (num_re * inv_den).reshape(b, l, K, H * M)
        im = (num_im * inv_den).reshape(b, l, K, H * M)
        mean_sq = (jnp.sum(jnp.square(re), -1) + jnp.sum(jnp.square(im), -1)) / (2.0 * H * M)
        rs = jax.lax.rsqrt(mean_sq[..., None] + 1e-05)
        y = re * rs * norm_scale[:H * M] @ W_re + im * rs * norm_scale[H * M:] @ W_im
        y = y.reshape(b, l, D)
        return y * x_gate @ out_proj_w

    def _L0_ffn_ref(x, gate_w, gate_b, w1, b1, w2, b2):
        import jax, jax.numpy as jnp
        import numpy as np
        B, S, D, H, E = (4, 256, 128, 512, 8)
        b, s, d = x.shape
        xf = x.reshape(-1, d)
        logits = xf @ gate_w.T + gate_b
        top1 = jnp.argmax(logits, axis=-1)
        out = jnp.zeros_like(xf)
        n_experts = w1.shape[0]
        for e in range(n_experts):
            h = jax.nn.relu(xf @ w1[e].T + b1[e])
            y = h @ w2[e].T + b2[e]
            out = out + jnp.where((top1 == e)[:, None], y, jnp.zeros((), y.dtype))
        return out.reshape(b, s, d)
    x = L0_attn_x
    x = x + 0.5 * _L0_ffn_ref(_layernorm(x, axis=-1), L0_ffn_gate_w, L0_ffn_gate_b, L0_ffn_w1, L0_ffn_b1, L0_ffn_w2, L0_ffn_b2)
    x = x + _L0_attn_ref(_layernorm(x, axis=-1), L0_attn_in_proj_w, L0_attn_conv_w, L0_attn_conv_b, L0_attn_theta, L0_attn_decay_slopes, L0_attn_anchor_slopes, L0_attn_score_scale, L0_attn_deriv_logits, L0_attn_norm_scale, L0_attn_W_re, L0_attn_W_im, L0_attn_out_proj_w)
    x = x + 0.5 * _L0_ffn_ref(_layernorm(x, axis=-1), L0_ffn_gate_w, L0_ffn_gate_b, L0_ffn_w1, L0_ffn_b1, L0_ffn_w2, L0_ffn_b2)
    return x

_drawn_inputs = setup_inputs


def setup_inputs(seed=0):
    import zlib

    import numpy as np

    out = dict(_drawn_inputs(seed))
    spreads = {'L0_attn_conv_b': (0.0, 0.1),
     'L0_attn_score_scale': (1.0, 0.6),
     'L0_attn_norm_scale': (1.0, 0.2)}
    factors = {'L0_attn_theta': 3.816, 'L0_attn_anchor_slopes': 64.0, 'L0_attn_W_im': 3.269}
    for name, (base, spread) in spreads.items():
        noise = np.random.default_rng([zlib.crc32(name.encode()), seed]).standard_normal(out[name].shape)
        drawn = base * np.exp(spread * noise) if base else spread * noise
        out[name] = jnp.asarray(drawn.astype(out[name].dtype))
    for name, factor in factors.items():
        out[name] = (out[name] * factor).astype(out[name].dtype)
    return out
```

```python
from contextlib import ExitStack

import numpy as np
import concourse.bass as bass
from concourse import mybir

F32 = mybir.dt.float32
BF16 = mybir.dt.bfloat16
I32 = mybir.dt.int32
ALU = mybir.AluOpType
ACT = mybir.ActivationFunctionType
AX = mybir.AxisListType

P = 128
L = 2048
D = 128
NT = L // P
GT = 4
NG = NT // GT
CH = GT * P
E = 8
HID = 512
HC = HID // P
NBLK = NT + E - 1
RING = 4
LEAD = 3
TURNS = (NBLK - LEAD - RING) // RING
K = 32
H = D // K
M = 4
A = 4
CK = 4
PAD = CK - 1
TOTAL = 2 * D + K
EPS = 1e-5
ROUND = 12582912.0
ROUND_POS = 8388608.0
TWO_PI = float(np.nextafter(np.float32(2 * np.pi), np.float32(0)))
RSQRT_SEED = float(0x5F3759DF)
S_DIV = 1.0 / (2.0 * H * M)


class Steps:

    def __init__(self, engine, semaphore):
        self.engine, self.semaphore, self.count = engine, semaphore, 0

    def did(self, instruction):
        self.count += 1
        instruction.then_inc(self.semaphore, 1)

    def wait(self):
        self.engine.wait_ge(self.semaphore, self.count)

    def then(self, instruction):
        self.did(instruction)
        self.wait()


def build(nc, x, gate_w, gate_b, w1, b1, w2, b2, in_w, conv_w, conv_b, theta, slopes, score_scale,
          deriv, norm_scale, w_reim, out_w, out):
    with ExitStack() as ctx:
        def sb(name, shape, dt=F32):
            return ctx.enter_context(nc.sbuf_tensor(name, shape, dt))

        def pb(name, shape=(P, 512), dt=F32):
            return ctx.enter_context(nc.psum_tensor(name, list(shape), dt))

        def sem(name):
            return ctx.enter_context(nc.semaphore(name))

        sorted_rows = nc.dram_tensor("sorted_rows", (NBLK * P, D), F32, kind="Internal").ap()
        slot_rows = nc.dram_tensor("slot_rows", (NBLK * P, D), F32, kind="Internal").ap()
        sorted_v = sorted_rows.rearrange("(b p) d -> p b d", p=P)
        slot_v = slot_rows.rearrange("(b p) d -> p b d", p=P)

        w1_sb = sb("w1_sb", [P, E, HID])
        w2_sb = sb("w2_sb", [P, E, HC, D])
        b1_sb = sb("b1_sb", [P, E, HID])
        b2_sb = sb("b2_sb", [P, E, D])
        gw_sb = sb("gw_sb", [P, E])
        gb_sb = sb("gb_sb", [P, E])
        inw_sb = sb("inw_sb", [P, TOTAL])
        cw_sb = sb("cw_sb", [P, CK, TOTAL])
        cbs_sb = sb("cbs_sb", [P, K])
        cbv_sb = sb("cbv_sb", [P, 2])
        th_sb = sb("th_sb", [P, M])
        sl_sb = sb("sl_sb", [P, K])
        ss_sb = sb("ss_sb", [P, K])
        dl_sb = sb("dl_sb", [P, 3])
        dmix = sb("dmix", [P, 8])
        ns_sb = sb("ns_sb", [P, 2, M])
        wri_sb = sb("wri_sb", [P, 2, M, H])
        wbd_sb = sb("wbd_sb", [P, 2 * M, K, H])
        ow_sb = sb("ow_sb", [P, D])
        ident = sb("ident", [P, P])
        head_mask = sb("head_mask", [P, K])
        before = sb("before", [P, P], BF16)
        ones_b = sb("ones_b", [P, P], BF16)
        first_tile = sb("first_tile", [P, E, NT])
        rev_e = sb("rev_e", [P, E])
        ones_e = sb("ones_e", [P, E])
        blk_no = sb("blk_no", [1, NBLK])
        zeros = sb("zeros", [P, D])
        half_pi = sb("half_pi", [P, 1])
        dist = sb("dist", [P, NT, K])
        tw = sb("tw", [P, NT, K])
        xr = sb("xr", [P, NT, D])
        xn = sb("xn", [P, NT, D])
        yg = sb("yg", [P, NT, D])
        rows = sb("rows", [P, RING, D])
        res = sb("res", [P, NBLK, D])
        st = sb("st", [P, GT, 6])
        ln = sb("ln", [P, 8, GT])
        lg = sb("lg", [P, E, NT])
        oh = sb("oh", [P, E, NT], BF16)
        rt = sb("rt", [P, 2, E, NT])
        re8 = sb("re8", [P, 4, E])
        mx = sb("mx", [P, NT])
        slot_i = sb("slot_i", [P, NT], I32)
        cmp_b = sb("cmp_b", [1, NBLK, E])
        exp_f = sb("exp_f", [1, NBLK])
        exp_i = sb("exp_i", [1, NBLK], I32)
        xT = sb("xT", [P, PAD + L])
        xsT = sb("xsT", [P, 2, P])
        hb = sb("hb", [P, 2, HID])
        hT = sb("hT", [P, 2, HID])
        sx = sb("sx", [P, NT, K])
        pw = yg[:, :, :].rearrange("p n (k h) -> p n k h", h=H)
        val = sb("val", [P, 2, CH])
        gate = sb("gate", [P, 2, CH])
        ub = sb("ub", [P, M, CH])
        vb = sb("vb", [P, M, CH])
        sn = res[:, 0:NT, :].rearrange("p n d -> p (n d)").rearrange("p (m t) -> p m t", m=M)
        cs = sb("cs", [P, M, CH])
        ga, g_sb = hb[:, 0, :], hb[:, 1, :]
        dmx, ygt = hT[:, 0, :], hT[:, 1, :]
        num = sb("num", [P, 2 * M + 1, CH])
        carry = sb("carry", [P, 2 * M + 1, 1])
        sq = sb("sq", [P, 2 * M + 1, CH])
        nw = sb("nw", [P, 4, P])
        rs = sb("rs", [P, GT, K, H])
        ln1 = sb("ln1", [P, 5, K])

        p_t = pb("p_t")
        p_m = pb("p_m")
        p_a = pb("p_a")
        p_b = pb("p_b")
        p_c = pb("p_c")
        p_d = pb("p_d")
        p_y = pb("p_y")
        p_x = pb("p_x")
        p_h, p_ht = (p_a, p_b), (p_c, p_d)
        p_xs, p_ys = (p_x, p_t), (p_y, p_m)
        LOG = p_m[:, 0:P].rearrange("p (n e) -> p n e", e=E)
        RANK = p_m[:, P:2 * P].rearrange("p (e n) -> p e n", e=E)
        TOT = p_m[:, 2 * P:3 * P].rearrange("p (e n) -> p e n", e=E)
        SQS = p_m[:, 3 * P:4 * P]

        s_x = [sem(f"s_x{g}") for g in range(NG)]
        s_small = sem("s_small")
        s_w1 = sem("s_w1")
        s_w2 = sem("s_w2")
        s_b = sem("s_b")
        s_zero = sem("s_zero")
        s_rows = [sem(f"s_rows{i}") for i in range(RING)]
        s_scat = sem("s_scat")
        s_store = sem("s_store")
        s_gat = [sem(f"s_gat{n}") for n in range(NG)]
        s_out = sem("s_out")
        const_ready = sem("const_ready")
        wz_ready = sem("wz_ready")
        wbd_ready = sem("wbd_ready")
        th_ready = sem("th_ready")
        pre_dve = sem("pre_dve")
        pre_act = sem("pre_act")
        xn_ready = sem("xn_ready")
        xt_done = sem("xt_done")
        xT_ready = sem("xT_ready")
        lg_done = sem("lg_done")
        oh_ready = sem("oh_ready")
        rank_done = sem("rank_done")
        slot_ready = sem("slot_ready")
        ids_ready = sem("ids_ready")
        tx_done = sem("tx_done")
        xsT_ready = sem("xsT_ready")
        h_done = sem("h_done")
        hb_ready = sem("hb_ready")
        th_done = sem("th_done")
        hT_ready = sem("hT_ready")
        y_done = sem("y_done")
        yb_ready = sem("yb_ready")
        x_ready = sem("x_ready")
        s_done = sem("s_done")
        sx_ready = sem("sx_ready")
        ex_ready = sem("ex_ready")
        pw_ready = sem("pw_ready")
        zv_done = sem("zv_done")
        zg_done = sem("zg_done")
        pwp_done = sem("pwp_done")
        pwp_used = sem("pwp_used")
        val_ready = sem("val_ready")
        gate_ready = sem("gate_ready")
        uv_ready = sem("uv_ready")
        r_ready = sem("r_ready")
        abs_ready = sem("abs_ready")
        sin_ready = sem("sin_ready")
        cos_ready = sem("cos_ready")
        g_ready = sem("g_ready")
        im_ready = sem("im_ready")
        re_ready = sem("re_ready")
        re_sums = sem("re_sums")
        im_sums = sem("im_sums")
        dmx_ready = sem("dmx_ready")
        sq_ready = sem("sq_ready")
        w_done = sem("w_done")
        sq_done = sem("sq_done")
        rs_ready = sem("rs_ready")
        rsp_done = sem("rsp_done")
        yt_ready = sem("yt_ready")
        o_done = sem("o_done")
        dve_step = sem("dve_step")
        pool_step = sem("pool_step")
        act_step = sem("act_step")
        N_SMALL = 14 * 16

        block = ctx.enter_context(nc.Block())

        @block.sync
        def _(sp):
            x_v = x.rearrange("(n p) d -> p n d", p=P)
            out_v = out.rearrange("(n p) d -> p n d", p=P)
            for g in range(NG):
                sp.dma_start(xr[:, GT * g:GT * (g + 1), :], x_v[:, GT * g:GT * (g + 1), :]).then_inc(s_x[g], 16)
            for dst, src in ((gw_sb[:, :], gate_w), (gb_sb[:, :], gate_b.broadcast_to([P, E])),
                             (inw_sb[:, :], in_w),
                             (cw_sb[:, :, :].rearrange("p a b -> p (a b)"), conv_w.broadcast_to([P, CK * TOTAL])),
                             (cbs_sb[:, :], conv_b[:, 2 * D:TOTAL].broadcast_to([P, K])),
                             (cbv_sb[:, 0:1], conv_b[:, 0:D].rearrange("a p -> p a")),
                             (cbv_sb[:, 1:2], conv_b[:, D:2 * D].rearrange("a p -> p a")),
                             (th_sb[:, :], theta), (sl_sb[:, :], slopes.broadcast_to([P, K])),
                             (ss_sb[:, :], score_scale.broadcast_to([P, K])),
                             (dl_sb[:, :], deriv.broadcast_to([P, 3])),
                             (ns_sb[:, :, :], norm_scale), (wri_sb[:, :, :, :], w_reim),
                             (ow_sb[:, :], out_w)):
                sp.dma_start(dst, src).then_inc(s_small, 16)
            sp.wait_ge(const_ready, 1)
            sp.dma_start(sorted_v, zeros[:, :].rearrange("p (a d) -> p a d", a=1).broadcast_to([P, NBLK, D])).then_inc(s_zero, 16)
            sp.dma_start(w1_sb[:, :, :], w1).then_inc(s_w1, 16)
            sp.dma_start(b1_sb[:, :, :].rearrange("p e h -> p (e h)"), b1.broadcast_to([P, E * HID])).then_inc(s_b, 16)
            sp.dma_start(w2_sb[:, :, :, :], w2).then_inc(s_w2, 16)
            sp.dma_start(b2_sb[:, :, :].rearrange("p e d -> p (e d)"), b2.broadcast_to([P, E * D])).then_inc(s_b, 16)

            def blocks(f):
                b0 = NBLK * f

                def load(b, r):
                    sp.dma_start(rows[:, r % RING, :], sorted_v[:, bass.ds(b, 1), :].rearrange("p a d -> p (a d)")).then_inc(s_rows[r % RING], 16)

                def store(b):
                    sp.wait_ge(yb_ready, b + b0 + 1)
                    sp.dma_start(slot_v[:, bass.ds(b, 1), :], res[:, bass.ds(b, 1), :]).then_inc(s_store, 16)

                def turn(b, r):
                    sp.wait_ge(tx_done, b + b0 - RING + 1)
                    load(b, r)
                    if r > RING:
                        store(b - RING - 1)

                sp.wait_ge(s_scat, 16 * NT * (f + 1))
                for b in range(RING):
                    load(b, b)
                for b in range(RING, RING + LEAD):
                    turn(b, b)
                with sp.Fori(0, TURNS) as t:
                    for r in range(RING + LEAD, 2 * RING + LEAD):
                        turn(t * RING + r, r)
                for b in range(NBLK - RING - 1, NBLK):
                    store(b)

            blocks(0)
            blocks(1)
            for g in range(NG):
                sp.wait_ge(x_ready, 2 * NG + g + 1)
                sp.dma_start(out_v[:, GT * g:GT * (g + 1), :], xr[:, GT * g:GT * (g + 1), :]).then_inc(s_out, 16)
            sp.wait_ge(s_out, 16 * NG)

        @block.gpsimd
        def _(pool):
            steps = Steps(pool, pool_step)
            g_ = nc.gpsimd
            g_.memset(zeros[:, :], 0.0).then_inc(const_ready, 1)
            steps.did(g_.memset(ident[:, :], 0.0))
            steps.did(g_.memset(half_pi[:, :], float(np.pi / 2)))
            steps.did(g_.memset(head_mask[:, :], 1.0))
            steps.did(g_.memset(before[:, :], 1.0))
            steps.did(g_.memset(ones_b[:, :], 1.0))
            steps.did(g_.memset(first_tile[:, :, :], 1.0))
            steps.did(g_.memset(ones_e[:, :], 1.0))
            steps.did(g_.memset(carry[:, :, :], 0.0))
            steps.did(g_.memset(xT[:, 0:PAD], 0.0))
            steps.did(g_.iota(rev_e[:, :], pattern=[[-1, E]], base=E, channel_multiplier=0, allow_small_or_imprecise_dtypes=True))
            steps.did(g_.iota(blk_no[:, :], pattern=[[1, NBLK]], base=0, channel_multiplier=0, allow_small_or_imprecise_dtypes=True))
            steps.did(g_.iota(dist[:, :, 0:K - A], pattern=[[-P, NT], [0, K - A]], base=L - 1, channel_multiplier=-1, allow_small_or_imprecise_dtypes=True))
            steps.did(g_.iota(dist[:, :, K - A:K], pattern=[[P, NT], [0, A]], base=0, channel_multiplier=1, allow_small_or_imprecise_dtypes=True))
            steps.wait()
            steps.did(g_.affine_select(out=ident[:, :], in_=ident[:, :], compare_op=ALU.not_equal, fill=1.0, base=0,
                                       pattern=[[-1, P]], channel_multiplier=1))
            steps.did(g_.affine_select(out=before[:, :], in_=before[:, :], compare_op=ALU.is_ge, fill=0.0, base=-1,
                                       pattern=[[1, P]], channel_multiplier=-1))
            steps.did(g_.memset(first_tile[:, :, 0:1], 0.0))
            steps.then(g_.affine_select(out=head_mask[:, :], in_=head_mask[:, :], compare_op=ALU.is_ge, fill=0.0, base=0,
                                        pattern=[[-H, K]], channel_multiplier=1))
            g_.affine_select(out=head_mask[:, :], in_=head_mask[:, :], compare_op=ALU.is_ge, fill=0.0, base=H - 1,
                             pattern=[[H, K]], channel_multiplier=-1).then_inc(const_ready, 1)
            pool.wait_ge(const_ready, 2)
            pool.wait_ge(s_small, N_SMALL)
            g_.tensor_tensor(cw_sb[:, :, :], cw_sb[:, :, :],
                             inw_sb[:, :].rearrange("p (a n) -> p a n", a=1).broadcast_to([P, CK, TOTAL]),
                             ALU.mult).then_inc(wz_ready, 1)
            g_.tensor_scalar(th_sb[:, :], th_sb[:, :], float(1 / (2 * np.pi)), 0.0, ALU.mult, ALU.add).then_inc(th_ready, 1)
            steps.then(g_.tensor_tensor(wri_sb[:, :, :, :], wri_sb[:, :, :, :],
                                        ns_sb[:, :, :].rearrange("p r (m a) -> p r m a", a=1).broadcast_to([P, 2, M, H]), ALU.mult))
            for i in range(2 * M):
                g_.tensor_tensor(wbd_sb[:, i, :, :],
                                 wri_sb[:, i // M, i % M, :].rearrange("p (a h) -> p a h", a=1).broadcast_to([P, K, H]),
                                 head_mask[:, :].rearrange("p (k a) -> p k a", a=1).broadcast_to([P, K, H]),
                                 ALU.mult).then_inc(wbd_ready, 1)

            def scatter(f):
                pool.wait_ge(slot_ready, f + 1)
                if f == 0:
                    pool.wait_ge(s_zero, 16)
                for n in range(NT):
                    g_.indirect_dma_start(out=sorted_rows[:, :], out_offset=bass.IndirectOffsetOnAxis(ap=slot_i[:, n:n + 1], axis=0),
                                          in_=xn[:, n, :], in_offset=None).then_inc(s_scat, 16)

            def gather(f):
                pool.wait_ge(s_store, 16 * NBLK * (f + 1))
                if f:
                    pool.wait_ge(x_ready, NG)
                for n in range(NT):
                    g_.indirect_dma_start(out=yg[:, n, :], out_offset=None, in_=slot_rows[:, :],
                                          in_offset=bass.IndirectOffsetOnAxis(ap=slot_i[:, n:n + 1], axis=0)).then_inc(s_gat[n // GT], 16)

            def phases(c):
                pool.wait_ge(val_ready, c + 1)
                pool.wait_ge(th_ready, 1)
                if c >= 1:
                    pool.wait_ge(sin_ready, c)
                    pool.wait_ge(cos_ready, c)
                for m in range(M):
                    g_.tensor_scalar(ub[:, m, :], val[:, c % 2, :], th_sb[:, m:m + 1], 0.0, ALU.mult, ALU.add).then_inc(uv_ready, 1)
                    g_.tensor_scalar(vb[:, m, :], val[:, c % 2, :], th_sb[:, m:m + 1], ROUND, ALU.mult, ALU.add).then_inc(uv_ready, 1)

            def imag(c):
                pool.wait_ge(g_ready, c + 1)
                pool.wait_ge(sin_ready, c + 1)
                if c >= 1:
                    pool.wait_ge(sq_ready, 3 * c)
                    pool.wait_ge(w_done, c)
                g_.tensor_tensor(num[:, M:2 * M, :], sn[:, :, :],
                                 g_sb.rearrange("p (a n) -> p a n", a=1).broadcast_to([P, M, CH]), ALU.mult).then_inc(im_ready, 1)

            scatter(0)
            gather(0)
            phases(0)
            for c in range(NG):
                imag(c)
                if c + 1 < NG:
                    phases(c + 1)
            scatter(1)
            gather(1)

        @block.scalar
        def _(act):
            steps = Steps(act, act_step)

            def to_free(q):
                g = q % NG
                act.wait_ge(xt_done, q + 1)
                nc.scalar.copy(xT[:, PAD + CH * g:PAD + CH * (g + 1)], p_t[:, :]).then_inc(xT_ready, 1)

            for g in range(NG):
                to_free(g)
            act.wait_ge(pre_dve, 1)
            nc.scalar.activation(ln1[:, 1, :], ln1[:, 0, :], ACT.Exp, scale=-1.0).then_inc(pre_act, 1)
            act.wait_ge(pre_dve, 2)
            nc.scalar.activation(dl_sb[:, :], dl_sb[:, :], ACT.Exp).then_inc(pre_act, 1)
            act.wait_ge(pre_dve, 3)
            nc.scalar.activation(tw[:, :, :], dist[:, :, :], ACT.Exp).then_inc(pre_act, 1)

            def blocks(f):
                b0 = NBLK * f

                def copy_x(b, r):
                    act.wait_ge(tx_done, b + b0 + 1)
                    if r + b0 >= 2:
                        act.wait_ge(h_done, b + b0 - 1)
                    nc.scalar.copy(xsT[:, r % 2, :], p_xs[r % 2][:, 0:P]).then_inc(xsT_ready, 1)

                def relu(b, r):
                    act.wait_ge(th_done, b + b0 + 1)
                    if r + b0 >= 2:
                        act.wait_ge(y_done, b + b0 - 1)
                    nc.scalar.activation(hT[:, r % 2, :], p_ht[r % 2][:, :], ACT.Relu).then_inc(hT_ready, 1)

                copy_x(0, 0)
                copy_x(1, 1)
                for b in range(LEAD):
                    copy_x(b + 2, b + 2)
                    relu(b, b)
                with act.Fori(0, TURNS) as t:
                    for r in range(LEAD, LEAD + RING):
                        copy_x(t * RING + (r + 2), r + 2)
                        relu(t * RING + r, r)
                for b in range(NBLK - RING, NBLK):
                    if b + 2 < NBLK:
                        copy_x(b + 2, b + 2)
                    relu(b, b)

            blocks(0)
            for g in range(NG):
                to_free(NG + g)
            act.wait_ge(sx_ready, 1)
            nc.scalar.activation(sx[:, :, :], sx[:, :, :], ACT.Exp).then_inc(ex_ready, 1)

            def front(c):
                act.wait_ge(zg_done, c + 1)
                if c >= 2:
                    act.wait_ge(yt_ready, c - 1)
                nc.scalar.activation(gate[:, c % 2, :], p_b[:, :], ACT.Silu, bias=cbv_sb[:, 1:2]).then_inc(gate_ready, 1)
                act.wait_ge(zv_done, c + 1)
                nc.scalar.activation(val[:, c % 2, :], p_a[:, :], ACT.Identity, bias=cbv_sb[:, 0:1]).then_inc(val_ready, 1)

            def trig(c):
                act.wait_ge(r_ready, c + 1)
                nc.scalar.activation(ub[:, :, :], vb[:, :, :], ACT.Abs).then_inc(abs_ready, 1)
                if c >= 1:
                    act.wait_ge(im_ready, c)
                nc.scalar.activation(sn[:, :, :], vb[:, :, :], ACT.Sin, scale=-TWO_PI).then_inc(sin_ready, 1)
                act.wait_ge(abs_ready, c + 1)
                if c >= 1:
                    act.wait_ge(re_ready, c)
                nc.scalar.activation(cs[:, :, :], ub[:, :, :], ACT.Sin, scale=-TWO_PI, bias=half_pi[:, :]).then_inc(cos_ready, 1)

            def squares(c):
                if c >= 1:
                    act.wait_ge(sq_done, c)
                act.wait_ge(re_sums, M * (c + 1))
                nc.scalar.activation(sq[:, 0:M, :], num[:, 0:M, :], ACT.Square).then_inc(sq_ready, 1)
                act.wait_ge(dmx_ready, c + 1)
                nc.scalar.activation(sq[:, 2 * M, :], dmx, ACT.Square, scale=float(np.sqrt(EPS / S_DIV / H))).then_inc(sq_ready, 1)
                act.wait_ge(im_sums, M * (c + 1))
                nc.scalar.activation(sq[:, M:2 * M, :], num[:, M:2 * M, :], ACT.Square).then_inc(sq_ready, 1)

            front(0)
            trig(0)
            for c in range(NG):
                if c + 1 < NG:
                    front(c + 1)
                squares(c)
                if c + 1 < NG:
                    trig(c + 1)
                to_free(2 * NG + c)
            blocks(1)

        @block.tensor
        def _(pe):
            mm = nc.tensor.matmul
            pe.wait_ge(const_ready, 2)

            def turn(q):
                pe.wait_ge(xn_ready, GT * (q + 1))
                if q >= 1:
                    pe.wait_ge(xT_ready, q)
                for n in range(GT):
                    last = nc.tensor.transpose(p_t[:, P * n:P * (n + 1)], xn[:, GT * (q % NG) + n, :], ident[:, :])
                last.then_inc(xt_done, 1)

            def logits(q):
                g = q % NG
                pe.wait_ge(xT_ready, q + 1)
                if q >= 2 * NG:
                    pe.wait_ge(slot_ready, 1)
                for n in range(GT * g, GT * (g + 1)):
                    last = mm(LOG[:, n, :], xT[:, PAD + P * n:PAD + P * (n + 1)], gw_sb[:, :], start=True, stop=True)
                last.then_inc(lg_done, 1)

            def ranks(f):
                pe.wait_ge(oh_ready, f + 1)
                oh_v = oh[:, :, :].rearrange("p e n -> p (e n)")
                mm(p_m[:, P:2 * P], before[:, :], oh_v, start=True, stop=True)
                mm(p_m[:, 2 * P:3 * P], ones_b[:, :], oh_v, start=True, stop=True).then_inc(rank_done, 1)

            def blocks(f):
                b0 = NBLK * f

                def turn_x(b, r):
                    loads = f * ((NBLK - r % RING + RING - 1) // RING) + r // RING + 1
                    pe.wait_ge(s_rows[r % RING], 16 * loads + (b - r) * (16 // RING))
                    if r + b0 >= 2:
                        pe.wait_ge(xsT_ready, b + b0 - 1)
                    nc.tensor.transpose(p_xs[r % 2][:, 0:P], rows[:, r % RING, :], ident[:, :]).then_inc(tx_done, 1)

                def hidden(b, r):
                    e = pe.value_load(exp_i[0:1, bass.ds(b, 1)], min_val=0, max_val=E - 1)
                    pe.wait_ge(xsT_ready, b + b0 + 1)
                    if r + b0 >= 2:
                        pe.wait_ge(hb_ready, b + b0 - 1)
                    mm(p_h[r % 2][:, :], xsT[:, r % 2, :], w1_sb[:, bass.ds(e, 1), :].rearrange("p a h -> p (a h)"),
                       start=True, stop=True).then_inc(h_done, 1)

                def turn_h(b, r):
                    pe.wait_ge(hb_ready, b + b0 + 1)
                    if r + b0 >= 2:
                        pe.wait_ge(hT_ready, b + b0 - 1)
                    for j in range(HC):
                        last = nc.tensor.transpose(p_ht[r % 2][:, P * j:P * (j + 1)], hb[:, r % 2, P * j:P * (j + 1)], ident[:, :])
                    last.then_inc(th_done, 1)

                def expert_out(b, r):
                    e = pe.value_load(exp_i[0:1, bass.ds(b, 1)], min_val=0, max_val=E - 1)
                    pe.wait_ge(hT_ready, b + b0 + 1)
                    if r + b0 >= 2:
                        pe.wait_ge(yb_ready, b + b0 - 1)
                    for j in range(HC):
                        last = mm(p_ys[r % 2][:, 0:P], hT[:, r % 2, P * j:P * (j + 1)],
                                  w2_sb[:, bass.ds(e, 1), j, :].rearrange("p a d -> p (a d)"),
                                  start=(j == 0), stop=(j == HC - 1))
                    last.then_inc(y_done, 1)

                pe.wait_ge(ids_ready, f + 1)
                turn_x(0, 0)
                turn_x(1, 1)
                pe.wait_ge(s_w1, 16)
                hidden(0, 0)
                pe.wait_ge(s_w2, 16)
                for b in range(LEAD):
                    turn_x(b + 2, b + 2)
                    hidden(b + 1, b + 1)
                    turn_h(b, b)
                    if b:
                        expert_out(b - 1, b - 1)
                with pe.Fori(0, TURNS) as t:
                    for r in range(LEAD, LEAD + RING):
                        turn_x(t * RING + (r + 2), r + 2)
                        hidden(t * RING + (r + 1), r + 1)
                        turn_h(t * RING + r, r)
                        expert_out(t * RING + (r - 1), r - 1)
                for b in range(NBLK - RING, NBLK):
                    if b + 2 < NBLK:
                        turn_x(b + 2, b + 2)
                    if b + 1 < NBLK:
                        hidden(b + 1, b + 1)
                    turn_h(b, b)
                    expert_out(b - 1, b - 1)
                expert_out(NBLK - 1, NBLK - 1)

            def scores():
                pe.wait_ge(wz_ready, 1)
                for n in range(NT):
                    for j in range(CK):
                        last = mm(p_x[:, K * n:K * (n + 1)], xT[:, P * n + j:P * n + j + P], cw_sb[:, j, 2 * D:TOTAL],
                                  start=(j == 0), stop=(j == CK - 1))
                last.then_inc(s_done, 1)

            def project(c):
                if c >= 1:
                    pe.wait_ge(gate_ready, c)
                for j in range(CK):
                    last = mm(p_b[:, :], cw_sb[:, j, D:2 * D], xT[:, CH * c + j:CH * c + j + CH], start=(j == 0), stop=(j == CK - 1))
                last.then_inc(zg_done, 1)
                if c >= 1:
                    pe.wait_ge(val_ready, c)
                for j in range(CK):
                    last = mm(p_a[:, :], cw_sb[:, j, 0:D], xT[:, CH * c + j:CH * c + j + CH], start=(j == 0), stop=(j == CK - 1))
                last.then_inc(zv_done, 1)

            def spread(dst, src):
                return nc.tensor.transpose(dst, src.rearrange("p k h -> p (k h)"), ident[:, :])

            def weights(c):
                pe.wait_ge(pw_ready, GT * (c + 1))
                if c >= 1:
                    pe.wait_ge(pwp_used, c)
                for n in range(GT):
                    last = spread(p_c[:, P * n:P * (n + 1)], pw[:, GT * c + n, :, :])
                last.then_inc(pwp_done, 1)

            def heads(c):
                if c >= 1:
                    pe.wait_ge(yt_ready, c)
                else:
                    pe.wait_ge(wbd_ready, 2 * M)
                for i in range(2 * M):
                    if i == 0:
                        pe.wait_ge(re_sums, M * (c + 1))
                    if i == M:
                        pe.wait_ge(im_sums, M * (c + 1))
                    last = mm(p_y[:, :], wbd_sb[:, i, :, :].rearrange("p k h -> p (k h)"), num[:, i, :],
                              start=(i == 0), stop=(i == 2 * M - 1))
                last.then_inc(w_done, 1)

            def square_sums(c):
                pe.wait_ge(sq_ready, 3 * (c + 1))
                if c >= 1:
                    pe.wait_ge(rs_ready, c)
                for n in range(GT):
                    for i in range(2 * M + 1):
                        last = mm(SQS[:, K * n:K * (n + 1)], sq[:, i, P * n:P * (n + 1)], head_mask[:, :],
                                  start=(i == 0), stop=(i == 2 * M))
                last.then_inc(sq_done, 1)

            def spread_rs(c):
                pe.wait_ge(rs_ready, c + 1)
                if c >= 1:
                    pe.wait_ge(yt_ready, c)
                for n in range(GT):
                    last = spread(p_d[:, P * n:P * (n + 1)], rs[:, n, :, :])
                last.then_inc(rsp_done, 1)

            def outputs(c):
                pe.wait_ge(yt_ready, c + 1)
                if c >= 1:
                    pe.wait_ge(x_ready, NG + c)
                for n in range(GT):
                    last = mm(p_x[:, P * n:P * (n + 1)], ygt[:, P * n:P * (n + 1)], ow_sb[:, :], start=True, stop=True)
                last.then_inc(o_done, 1)

            pe.wait_ge(s_small, N_SMALL)
            for q in range(NG):
                turn(q)
                logits(q)
            ranks(0)
            blocks(0)
            for q in range(NG, 2 * NG):
                turn(q)
            pe.wait_ge(xT_ready, 2 * NG)
            scores()
            project(0)
            weights(0)
            for c in range(NG):
                if c + 1 < NG:
                    project(c + 1)
                    weights(c + 1)
                heads(c)
                square_sums(c)
                spread_rs(c)
                outputs(c)
                turn(2 * NG + c)
                logits(2 * NG + c)
            ranks(1)
            blocks(1)

        @block.vector
        def _(dve):
            steps = Steps(dve, dve_step)
            v = nc.vector
            ts, tt, stt = v.tensor_scalar, v.tensor_tensor, v.scalar_tensor_tensor

            def over(ap, n):
                return ap.rearrange("p (a m) -> p a m", a=1).broadcast_to([ap.shape[0], n, ap.shape[1]])

            def each(ap, n):
                return ap.rearrange("p (m a) -> p m a", a=1).broadcast_to([ap.shape[0], ap.shape[1], n])

            def rsqrt(y, a, t):
                steps.then(ts(y.bitcast(I32), a.bitcast(I32), -0.5, RSQRT_SEED, ALU.mult, ALU.add))
                for _ in range(3):
                    steps.then(stt(t, y, -0.5, y, ALU.mult, ALU.mult))
                    steps.then(tt(t, t, a, ALU.mult))
                    steps.then(stt(y, t, 1.5, y, ALU.add, ALU.mult))

            def half_sum(g, f):
                dve.wait_ge(s_gat[g], 16 * GT * (f + 1))
                t = slice(GT * g, GT * (g + 1))
                stt(xr[:, t, :], yg[:, t, :], 0.5, xr[:, t, :], ALU.mult, ALU.add).then_inc(x_ready, 1)

            def norm(q):
                g = q % NG
                for n in range(GT):
                    steps.did(v.bn_stats(st[:, n, :], xr[:, GT * g + n, :]))
                steps.wait()
                steps.did(tt(ln[:, 0, :], st[:, :, 1], st[:, :, 4], ALU.subtract))
                steps.did(tt(ln[:, 1, :], st[:, :, 1], st[:, :, 4], ALU.add))
                steps.then(tt(ln[:, 2, :], st[:, :, 2], st[:, :, 5], ALU.add))
                steps.did(stt(ln[:, 3, :], ln[:, 0, :], 0.25, ln[:, 0, :], ALU.mult, ALU.mult))
                steps.then(ts(ln[:, 4, :], ln[:, 1, :], 0.5, None, ALU.mult))
                steps.then(stt(ln[:, 5, :], ln[:, 2, :], 1.0 / D, ln[:, 3, :], ALU.mult, ALU.add))
                steps.then(ts(ln[:, 5, :], ln[:, 5, :], EPS, None, ALU.add))
                rsqrt(ln[:, 6, :], ln[:, 5, :], ln[:, 7, :])
                if q == NG:
                    dve.wait_ge(s_scat, 16 * NT)
                    dve.wait_ge(xt_done, NG)
                if q >= 2 * NG:
                    dve.wait_ge(xt_done, 2 * NG)
                for n in range(GT):
                    ts(xn[:, GT * g + n, :], xr[:, GT * g + n, :], ln[:, 4, n:n + 1], ln[:, 6, n:n + 1],
                       ALU.subtract, ALU.mult).then_inc(xn_ready, 1)
                dve.wait_ge(xn_ready, GT * (q + 1))

            def route(f):
                dve.wait_ge(lg_done, NG * (f + 1))
                by_token = lg[:, :, :].rearrange("p e n -> p n e")
                steps.then(tt(by_token, LOG, over(gb_sb[:, :], NT), ALU.add))
                steps.then(v.tensor_reduce(mx[:, :], by_token, AX.X, ALU.max))
                steps.then(tt(rt[:, 0, :, :], lg[:, :, :], over(mx[:, :], E), ALU.is_equal))
                steps.then(tt(rt[:, 0, :, :], rt[:, 0, :, :], each(rev_e[:, :], NT), ALU.mult))
                steps.then(v.tensor_reduce(mx[:, :], rt[:, 0, :, :].rearrange("p e n -> p n e"), AX.X, ALU.max))
                tt(oh[:, :, :], rt[:, 0, :, :], over(mx[:, :], E), ALU.is_equal).then_inc(oh_ready, 1)
                dve.wait_ge(rank_done, f + 1)
                steps.then(v.tensor_tensor_scan(rt[:, 1, :, :].rearrange("p e n -> p (e n)"),
                                                first_tile[:, :, :].rearrange("p e n -> p (e n)"),
                                                p_m[:, 2 * P:3 * P], 0.0, ALU.mult, ALU.add))
                steps.did(tt(rt[:, 0, :, :], rt[:, 1, :, :], TOT, ALU.subtract))
                steps.then(ts(re8[:, 0, :], rt[:, 1, :, NT - 1], 1.0 / P, 0.5 - 1.0 / (2 * P), ALU.mult, ALU.add))
                steps.did(tt(rt[:, 0, :, :], rt[:, 0, :, :], RANK, ALU.add))
                steps.then(ts(re8[:, 0, :], re8[:, 0, :], ROUND_POS, ROUND_POS, ALU.add, ALU.subtract))
                steps.then(v.tensor_tensor_scan(re8[:, 1, :], ones_e[:, :], re8[:, 0, :], 0.0, ALU.mult, ALU.add))
                steps.did(tt(cmp_b[:, :, :], each(blk_no[:, :], E), over(re8[0:1, 1, :], NBLK), ALU.is_ge))
                steps.then(tt(re8[:, 2, :], re8[:, 1, :], re8[:, 0, :], ALU.subtract))
                steps.then(stt(rt[:, 0, :, :], each(re8[:, 2, :], NT), float(P), rt[:, 0, :, :], ALU.mult, ALU.add))
                steps.then(tt(rt[:, 0, :, :], rt[:, 0, :, :], oh[:, :, :], ALU.mult))
                steps.then(v.tensor_reduce(mx[:, :], rt[:, 0, :, :].rearrange("p e n -> p n e"), AX.X, ALU.add))
                v.tensor_copy(slot_i[:, :], mx[:, :]).then_inc(slot_ready, 1)
                steps.then(v.tensor_reduce(exp_f[:, :], cmp_b[:, :, :], AX.X, ALU.add))
                ts(exp_i[:, :], exp_f[:, :], float(E - 1), None, ALU.min).then_inc(ids_ready, 1)
                dve.wait_ge(ids_ready, f + 1)

            def blocks(f):
                b0 = NBLK * f

                def add_b1(b, r):
                    e = dve.value_load(exp_i[0:1, bass.ds(b, 1)], min_val=0, max_val=E - 1)
                    dve.wait_ge(h_done, b + b0 + 1)
                    if r + b0 >= 2:
                        dve.wait_ge(th_done, b + b0 - 1)
                    tt(hb[:, r % 2, :], p_h[r % 2][:, :], b1_sb[:, bass.ds(e, 1), :].rearrange("p a h -> p (a h)"),
                       ALU.add).then_inc(hb_ready, 1)

                def add_b2(b, r):
                    e = dve.value_load(exp_i[0:1, bass.ds(b, 1)], min_val=0, max_val=E - 1)
                    dve.wait_ge(y_done, b + b0 + 1)
                    tt(res[:, bass.ds(b, 1), :].rearrange("p a d -> p (a d)"), p_ys[r % 2][:, 0:P],
                       b2_sb[:, bass.ds(e, 1), :].rearrange("p a d -> p (a d)"), ALU.add).then_inc(yb_ready, 1)

                if f == 0:
                    dve.wait_ge(s_b, 32)
                else:
                    dve.wait_ge(s_store, 16 * NBLK)
                add_b1(0, 0)
                for b in range(LEAD):
                    add_b1(b + 1, b + 1)
                    if b:
                        add_b2(b - 1, b - 1)
                with dve.Fori(0, TURNS) as t:
                    for r in range(LEAD, LEAD + RING):
                        add_b1(t * RING + (r + 1), r + 1)
                        add_b2(t * RING + (r - 1), r - 1)
                for b in range(NBLK - RING, NBLK):
                    if b + 1 < NBLK:
                        add_b1(b + 1, b + 1)
                    add_b2(b - 1, b - 1)
                add_b2(NBLK - 1, NBLK - 1)

            def prelude():
                dve.wait_ge(s_small, N_SMALL)
                dve.wait_ge(const_ready, 2)
                ts(ln1[:, 0, :].bitcast(I32), sl_sb[:, :].bitcast(I32), 0x7FFFFFFF, None, ALU.bitwise_and).then_inc(pre_dve, 1)
                steps.then(v.tensor_reduce(dmix[:, 0:1], dl_sb[:, :], AX.X, ALU.max))
                ts(dl_sb[:, :], dl_sb[:, :], dmix[:, 0:1], None, ALU.subtract).then_inc(pre_dve, 1)
                dve.wait_ge(pre_act, 1)
                steps.then(ts(ln1[:, 2, :], ln1[:, 1, :], 2.0, None, ALU.add))
                steps.then(v.reciprocal(ln1[:, 2, :], ln1[:, 2, :]))
                steps.then(tt(ln1[:, 1, :], ln1[:, 1, :], ln1[:, 2, :], ALU.mult))
                steps.then(tt(ln1[:, 2, :], ln1[:, 1, :], ln1[:, 1, :], ALU.mult))
                steps.then(ts(ln1[:, 3, :], ln1[:, 2, :], 1.0 / 15, None, ALU.mult))
                for n in range(13, 1, -2):
                    steps.then(stt(ln1[:, 3, :], ln1[:, 3, :], 1.0 / n, ln1[:, 2, :], ALU.add, ALU.mult))
                steps.then(stt(ln1[:, 3, :], ln1[:, 3, :], 1.0, ln1[:, 1, :], ALU.add, ALU.mult))
                steps.then(ts(ln1[:, 4, :], sl_sb[:, :], 0.0, None, ALU.max))
                steps.then(stt(ln1[:, 0, :], ln1[:, 3, :], 2.0, ln1[:, 4, :], ALU.mult, ALU.add))
                steps.then(ts(ln1[:, 0, :], ln1[:, 0, :], -1.0, None, ALU.mult))
                tt(dist[:, :, :], dist[:, :, :], over(ln1[:, 0, :], NT), ALU.mult).then_inc(pre_dve, 1)
                dve.wait_ge(pre_act, 2)
                steps.then(v.tensor_reduce(dmix[:, 1:2], dl_sb[:, :], AX.X, ALU.add))
                steps.then(v.reciprocal(dmix[:, 2:3], dmix[:, 1:2]))
                steps.then(ts(dmix[:, 3:6], dl_sb[:, :], dmix[:, 2:3], None, ALU.mult))
                steps.then(ts(dmix[:, 6:7], dmix[:, 5:6], -1.0, None, ALU.mult))

            def score_weights():
                dve.wait_ge(s_done, 1)
                steps.then(tt(sx[:, :, :], p_x[:, :].rearrange("p (n k) -> p n k", k=K), over(cbs_sb[:, :], NT), ALU.add))
                steps.then(tt(sx[:, :, :], sx[:, :, :], over(ss_sb[:, :], NT), ALU.mult))
                ts(sx[:, :, :], sx[:, :, :], -20.0, 20.0, ALU.max, ALU.min).then_inc(sx_ready, 1)
                dve.wait_ge(ex_ready, 1)
                dve.wait_ge(pre_act, 3)
                for n in range(NT):
                    tt(pw[:, n, :, :], each(sx[:, n, :], H), each(tw[:, n, :], H), ALU.mult).then_inc(pw_ready, 1)

            def reduce_phase(c):
                dve.wait_ge(uv_ready, 2 * M * (c + 1))
                stt(vb[:, :, :], vb[:, :, :], ROUND, ub[:, :, :], ALU.subtract, ALU.subtract).then_inc(r_ready, 1)

            def envelope(c):
                x_c = val[:, c % 2, :]
                dve.wait_ge(val_ready, c + 1)
                steps.then(ts(ga, x_c, dmix[:, 6:7], dmix[:, 4:5], ALU.mult, ALU.add))
                steps.then(tt(ga, ga, x_c, ALU.mult))
                dve.wait_ge(pwp_done, c + 1)
                if c >= 1:
                    dve.wait_ge(im_ready, c)
                    dve.wait_ge(re_ready, c)
                stt(g_sb, ga, dmix[:, 3:4], p_c[:, :], ALU.add, ALU.mult).then_inc(g_ready, 1)
                v.tensor_tensor_scan(num[:, 2 * M, :], p_c[:, :], ga, carry[:, 2 * M, :], ALU.add, ALU.bypass).then_inc(pwp_used, 1)
                dve.wait_ge(pwp_used, c + 1)
                if c >= 1:
                    dve.wait_ge(sq_ready, 3 * c)
                ts(dmx, num[:, 2 * M, :], 1e-4, None, ALU.max).then_inc(dmx_ready, 1)

            def running_sums(c):
                dve.wait_ge(cos_ready, c + 1)
                dve.wait_ge(g_ready, c + 1)
                if c >= 1:
                    dve.wait_ge(sq_ready, 3 * c)
                    dve.wait_ge(w_done, c)
                tt(num[:, 0:M, :], cs[:, :, :], over(g_sb, M), ALU.mult).then_inc(re_ready, 1)
                dve.wait_ge(re_ready, c + 1)
                for m in range(M):
                    v.tensor_tensor_scan(num[:, m, :], num[:, m, :], num[:, m, :], carry[:, m, :], ALU.add, ALU.bypass).then_inc(re_sums, 1)
                dve.wait_ge(im_ready, c + 1)
                for m in range(M, 2 * M):
                    v.tensor_tensor_scan(num[:, m, :], num[:, m, :], num[:, m, :], carry[:, m, :], ALU.add, ALU.bypass).then_inc(im_sums, 1)
                dve.wait_ge(re_sums, M * (c + 1))
                dve.wait_ge(im_sums, M * (c + 1))
                steps.then(v.tensor_copy(carry[:, :, :], num[:, :, CH - 1:CH]))

            def scale(c):
                dve.wait_ge(sq_done, c + 1)
                steps.then(ts(nw[:, 0, :], SQS, S_DIV, None, ALU.mult))
                if c >= 1:
                    dve.wait_ge(rsp_done, c)
                rsqrt(nw[:, 1, :], nw[:, 0, :], nw[:, 2, :])
                v.tensor_copy(rs[:, :, :, :].rearrange("p n k h -> p (n k) h"), each(nw[:, 1, :], H)).then_inc(rs_ready, 1)

            def gated(c):
                dve.wait_ge(rsp_done, c + 1)
                dve.wait_ge(gate_ready, c + 1)
                if c >= 1:
                    dve.wait_ge(o_done, c)
                steps.then(tt(ygt, gate[:, c % 2, :], p_d[:, :], ALU.mult))
                dve.wait_ge(w_done, c + 1)
                tt(ygt, ygt, p_y[:, :], ALU.mult).then_inc(yt_ready, 1)

            def add_heads(c):
                dve.wait_ge(o_done, c + 1)
                t = slice(GT * c, GT * (c + 1))
                tt(xr[:, t, :], xr[:, t, :], p_x[:, :].rearrange("p (n d) -> p n d", d=D), ALU.add).then_inc(x_ready, 1)

            for g in range(NG):
                dve.wait_ge(s_x[g], 16)
                norm(g)
            route(0)
            prelude()
            blocks(0)
            for g in range(NG):
                half_sum(g, 0)
                dve.wait_ge(x_ready, g + 1)
                norm(NG + g)
            score_weights()
            reduce_phase(0)
            envelope(0)
            for c in range(NG):
                running_sums(c)
                if c + 1 < NG:
                    reduce_phase(c + 1)
                    envelope(c + 1)
                scale(c)
                gated(c)
                add_heads(c)
                dve.wait_ge(x_ready, NG + c + 1)
                norm(2 * NG + c)
            route(1)
            blocks(1)
            for g in range(NG):
                half_sum(g, 1)


def kernel(**inputs):
    import concourse.bacc as _bacc
    from concourse.bass_utils import run_bass_kernel_spmd as _run

    a = {k.removeprefix("L0_"): np.asarray(v) for k, v in inputs.items()}
    wri = np.stack([a["attn_W_re"].reshape(H, M, H), a["attn_W_im"].reshape(H, M, H)], axis=1)
    ns = a["attn_norm_scale"].reshape(2, H, M).transpose(1, 0, 2)
    arrays = {
        "x": a["attn_x"].reshape(L, D),
        "gate_w": a["ffn_gate_w"].T,
        "gate_b": a["ffn_gate_b"].reshape(1, E),
        "w1": a["ffn_w1"].transpose(2, 0, 1),
        "b1": a["ffn_b1"].reshape(1, E * HID),
        "w2": a["ffn_w2"].reshape(E, D, HC, P).transpose(3, 0, 2, 1),
        "b2": a["ffn_b2"].reshape(1, E * D),
        "in_w": a["attn_in_proj_w"],
        "conv_w": a["attn_conv_w"].reshape(1, CK * TOTAL),
        "conv_b": a["attn_conv_b"].reshape(1, TOTAL),
        "theta": a["attn_theta"].reshape(K * H, M),
        "slopes": np.concatenate([a["attn_decay_slopes"], a["attn_anchor_slopes"]]).reshape(1, K),
        "score_scale": a["attn_score_scale"].reshape(1, K),
        "deriv": a["attn_deriv_logits"].reshape(1, 3),
        "norm_scale": np.broadcast_to(ns, (K, H, 2, M)).reshape(P, 2, M),
        "w_reim": np.broadcast_to(wri, (K, H, 2, M, H)).reshape(P, 2, M, H),
        "out_w": a["attn_out_proj_w"],
    }
    arrays = {k: np.ascontiguousarray(v) for k, v in arrays.items()}
    nc = _bacc.Bacc("TRN2", target_bir_lowering=False, num_devices=1)
    args = [nc.dram_tensor(f"in_{k}", v.shape, mybir.dt.from_np(v.dtype), kind="ExternalInput").ap()
            for k, v in arrays.items()]
    out = nc.dram_tensor("out_x", (L, D), F32, kind="ExternalOutput").ap()
    build(nc, *args, out)
    r = _run(nc, [{f"in_{k}": v for k, v in arrays.items()}], core_ids=[0])
    return r.results[0]["out_x"].reshape(1, L, D)
```

```python
from contextlib import ExitStack

import numpy as np
import concourse.bass as bass
from concourse import mybir

F32 = mybir.dt.float32
BF16 = mybir.dt.bfloat16
I32 = mybir.dt.int32
ALU = mybir.AluOpType
ACT = mybir.ActivationFunctionType
AX = mybir.AxisListType

P = 128
L = 2048
D = 128
NT = L // P
GT = 4
NG = NT // GT
CH = GT * P
E = 8
HID = 512
HC = HID // P
NBLK = NT + E - 1
RING = 6
LEAD = 3
TURNS = (NBLK - LEAD) // RING
TAIL = LEAD + TURNS * RING
K = 32
H = D // K
M = 4
A = 4
CK = 4
PAD = CK - 1
TOTAL = 2 * D + K
EPS = 1e-5
ROUND = 12582912.0
ROUND_POS = 8388608.0
TWO_PI = float(np.nextafter(np.float32(2 * np.pi), np.float32(0)))
RSQRT_SEED = float(0x5F3759DF)
S_DIV = 1.0 / (2.0 * H * M)


class Steps:

    def __init__(self, engine, semaphore):
        self.engine, self.semaphore, self.count = engine, semaphore, 0

    def did(self, instruction):
        self.count += 1
        instruction.then_inc(self.semaphore, 1)

    def wait(self):
        self.engine.wait_ge(self.semaphore, self.count)

    def then(self, instruction):
        self.did(instruction)
        self.wait()


def build(nc, x, gate_w, gate_b, w1, b1, w2, b2, in_w, conv_w, conv_b, theta, score_par, deriv,
          norm_scale, w_reim, out_w, out):
    with ExitStack() as ctx:
        def sb(name, shape, dt=F32):
            return ctx.enter_context(nc.sbuf_tensor(name, shape, dt))

        def pb(name, shape=(P, 512), dt=F32):
            return ctx.enter_context(nc.psum_tensor(name, list(shape), dt))

        def sem(name):
            return ctx.enter_context(nc.semaphore(name))

        pairs = nc.dram_tensor("pairs", (L, 2 * D), F32, kind="Internal").ap()
        x1_rows = nc.dram_tensor("x1_rows", (L, D), F32, kind="Internal").ap()
        pairs_v = pairs.rearrange("(n p) (i d) -> p n i d", p=P, i=2)

        w1_sb = sb("w1_sb", [P, E, HID])
        w2_sb = sb("w2_sb", [P, E, HC, D])
        b1_sb = sb("b1_sb", [P, E, HID])
        b2_sb = sb("b2_sb", [P, E, D])
        gw_sb = sb("gw_sb", [P, E])
        gb_sb = sb("gb_sb", [P, E])
        inw_sb = sb("inw_sb", [P, TOTAL])
        cw_sb = sb("cw_sb", [P, CK, 2 * D])
        cbv_sb = sb("cbv_sb", [P, 2])
        th_sb = sb("th_sb", [P, M])
        sp_sb = sb("sp_sb", [P, CK + 3])
        dl_sb = sb("dl_sb", [P, 3])
        dmix = sb("dmix", [P, 8])
        ns_sb = sb("ns_sb", [P, 2, M])
        wri_sb = sb("wri_sb", [P, 2, M, H])
        wbd_sb = sb("wbd_sb", [P, 2 * M, K, H])
        ow_sb = sb("ow_sb", [P, D])
        ident = sb("ident", [P, P])
        head_mask = sb("head_mask", [P, K])
        before = sb("before", [P, P], BF16)
        ones_b = sb("ones_b", [P, P], BF16)
        first_tile = sb("first_tile", [P, E, NT])
        rev_e = sb("rev_e", [P, E])
        ones_e = sb("ones_e", [P, E])
        blk_no = sb("blk_no", [P, NBLK])
        tok_no = sb("tok_no", [P, 1])
        tile_no = sb("tile_no", [P, NT])
        slot_no = sb("slot_no", [P, P], BF16)
        no_tok = sb("no_tok", [P, NBLK])
        half_pi = sb("half_pi", [P, 1])
        round_c = sb("round_c", [P, 1])
        expand = sb("expand", [P, P])
        tw = sb("tw", [P, CH])
        anchor = sb("anchor", [P, 4])
        head_i = sb("head_i", [P, 1], I32)
        xr = sb("xr", [P, NT, D])
        xn = sb("xn", [P, NT, D])
        rows = sb("rows", [P, RING, 2, D])
        res = sb("res", [P, NBLK, D])
        st = sb("st", [P, NT, 6])
        ln = sb("ln", [P, 8, NT])
        lg = sb("lg", [P, E, NT])
        oh = sb("oh", [P, E, NT], BF16)
        rt = sb("rt", [P, 2, E, NT])
        re8 = sb("re8", [P, 4, E])
        mx = sb("mx", [P, NT])
        slot_b = sb("slot_b", [P, 2, NT])
        inv = sb("inv", [P, 2, NBLK])
        tok_i = sb("tok_i", [P, NBLK], I32)
        cmp_b = sb("cmp_b", [1, NBLK, E])
        exp_f = sb("exp_f", [1, NBLK])
        exp_i = sb("exp_i", [1, NBLK], I32)
        xT = sb("xT", [P, PAD + L])
        xsT = sb("xsT", [P, 2, P])
        hb = sb("hb", [P, 2, HID])
        hT = sb("hT", [P, 2, HID])
        zs = sb("zs", [P, PAD + CH])
        sx = sb("sx", [P, CH])
        pw = sx
        val = sb("val", [P, 2, CH])
        gate = sb("gate", [P, NG, CH])
        in_blk = val[:, :, :].rearrange("p i n -> p (i n)").bitcast(BF16)[:, 0:NT * 3 * NBLK].rearrange(
            "p (n i b) -> p n i b", i=3, b=NBLK)
        ub = sb("ub", [P, M, CH])
        vb = sb("vb", [P, M, CH])
        sn = res[:, 0:NT, :].rearrange("p n d -> p (n d)").rearrange("p (m t) -> p m t", m=M)
        cs = sb("cs", [P, M, CH])
        pos = hT[:, 0, :]
        ga, g_sb = hb[:, 0, :], hb[:, 1, :]
        dmx, ygt = hT[:, 0, :], hT[:, 1, :]
        imb = sb("imb", [P, M, CH])
        num = sb("num", [P, 2 * M + 1, CH])
        carry = sb("carry", [P, 2 * M + 1, 1])
        sq = sb("sq", [P, 2 * M + 1, CH])
        nw = sb("nw", [P, 3, P + GT])
        rs = rows[:, 0:2, :, :].rearrange("p r i (k h) -> p (r i) k h", h=H)
        ln1 = sb("ln1", [P, 5])

        p_t = pb("p_t")
        p_m = pb("p_m")
        p_a = pb("p_a")
        p_b = pb("p_b")
        p_c = pb("p_c")
        p_d = pb("p_d")
        p_y = pb("p_y")
        p_x = pb("p_x")
        in_slot = hb[:, :, :].rearrange("p i n -> p (i n)").bitcast(BF16).rearrange("p (n s) -> p n s", s=P)
        INV = p_c[:, 0:2 * NBLK].rearrange("p (i b) -> p i b", b=NBLK)
        p_h, p_ht = (p_a, p_b), (p_c, p_d)
        p_xs, p_ys = (p_x, p_t), (p_y, p_m)
        p_hd = (p_y, p_x)
        p_turned = lambda q: p_x if q < NG and q % 2 else p_t
        LOG = p_m[:, 0:P].rearrange("p (n e) -> p n e", e=E)
        RANK = p_m[:, P:2 * P].rearrange("p (e n) -> p e n", e=E)
        TOT = p_m[:, 2 * P:3 * P].rearrange("p (e n) -> p e n", e=E)
        SQS = p_m[:, 3 * P:4 * P]

        s_x = [sem(f"s_x{g}") for g in range(NG)]
        s_small = sem("s_small")
        s_w1 = sem("s_w1")
        s_w2 = sem("s_w2")
        s_b = sem("s_b")
        s_pairs = sem("s_pairs")
        s_x1 = [sem(f"s_x1{g}") for g in range(NG)]
        s_rows = [sem(f"s_rows{i}") for i in range(RING)]
        s_scat = sem("s_scat")
        const_ready = sem("const_ready")
        wz_ready = sem("wz_ready")
        wbd_ready = sem("wbd_ready")
        th_ready = sem("th_ready")
        pre_dve = sem("pre_dve")
        pre_act = sem("pre_act")
        xn_ready = sem("xn_ready")
        xt_done = sem("xt_done")
        xT_ready = sem("xT_ready")
        lg_done = sem("lg_done")
        oh_ready = sem("oh_ready")
        rank_done = sem("rank_done")
        slot_ready = sem("slot_ready")
        in_blk_ready = sem("in_blk_ready")
        in_slot_ready = sem("in_slot_ready")
        inv_done = sem("inv_done")
        tok_ready = sem("tok_ready")
        b2_ready = sem("b2_ready")
        ids_ready = sem("ids_ready")
        tx_done = sem("tx_done")
        xsT_ready = sem("xsT_ready")
        h_done = sem("h_done")
        hb_ready = sem("hb_ready")
        th_done = sem("th_done")
        hT_ready = sem("hT_ready")
        y_done = sem("y_done")
        xb_ready = sem("xb_ready")
        yb_ready = sem("yb_ready")
        x_ready = sem("x_ready")
        zs_ready = sem("zs_ready")
        dmix_ready = sem("dmix_ready")
        s_done = sem("s_done")
        sx_ready = sem("sx_ready")
        ex_ready = sem("ex_ready")
        pw_ready = sem("pw_ready")
        zv_done = sem("zv_done")
        zg_done = sem("zg_done")
        pwp_done = sem("pwp_done")
        pwp_used = sem("pwp_used")
        val_ready = sem("val_ready")
        gate_ready = sem("gate_ready")
        u_ready = sem("u_ready")
        v_ready = sem("v_ready")
        poly_ready = sem("poly_ready")
        sqs_ready = sem("sqs_ready")
        r_ready = sem("r_ready")
        abs_ready = sem("abs_ready")
        sin_ready = sem("sin_ready")
        cos_ready = sem("cos_ready")
        g_ready = sem("g_ready")
        im_ready = sem("im_ready")
        re_ready = sem("re_ready")
        re_sums = sem("re_sums")
        im_sums = sem("im_sums")
        dmx_ready = sem("dmx_ready")
        sq_ready = sem("sq_ready")
        w_done = sem("w_done")
        sq_done = sem("sq_done")
        rs_ready = sem("rs_ready")
        rsp_done = sem("rsp_done")
        yt_ready = sem("yt_ready")
        o_done = sem("o_done")
        dve_step = sem("dve_step")
        pool_step = sem("pool_step")
        act_step = sem("act_step")
        N_SMALL = 12 * 16

        block = ctx.enter_context(nc.Block())

        @block.sync
        def _(sp):
            x_v = x.rearrange("(n p) d -> p n d", p=P)
            x1_v = x1_rows.rearrange("(n p) d -> p n d", p=P)
            for g in range(NG):
                sp.dma_start(xr[:, GT * g:GT * (g + 1), :], x_v[:, GT * g:GT * (g + 1), :]).then_inc(s_x[g], 16)
            for dst, src in ((gw_sb[:, :], gate_w), (gb_sb[:, :], gate_b.broadcast_to([P, E])),
                             (inw_sb[:, :], in_w),
                             (cw_sb[:, :, :].rearrange("p a b -> p (a b)"), conv_w.broadcast_to([P, CK * 2 * D])),
                             (cbv_sb[:, 0:1], conv_b[:, 0:D].rearrange("a p -> p a")),
                             (cbv_sb[:, 1:2], conv_b[:, D:2 * D].rearrange("a p -> p a")),
                             (th_sb[:, :], theta), (sp_sb[:, :], score_par),
                             (dl_sb[:, :], deriv.broadcast_to([P, 3])),
                             (ns_sb[:, :, :], norm_scale), (wri_sb[:, :, :, :], w_reim),
                             (ow_sb[:, :], out_w)):
                sp.dma_start(dst, src).then_inc(s_small, 16)
            sp.dma_start(w1_sb[:, :, :], w1).then_inc(s_w1, 16)
            sp.dma_start(b1_sb[:, :, :].rearrange("p e h -> p (e h)"), b1.broadcast_to([P, E * HID])).then_inc(s_b, 16)
            sp.dma_start(b2_sb[:, :, :].rearrange("p e d -> p (e d)"), b2.broadcast_to([P, E * D])).then_inc(s_b, 16)

            def store_pairs(f):
                for g in range(NG):
                    t = slice(GT * g, GT * (g + 1))
                    if f == 0:
                        sp.wait_ge(s_x[g], 16)
                        sp.wait_ge(xn_ready, GT * (g + 1))
                    else:
                        sp.wait_ge(x_ready, g + 1)
                        sp.wait_ge(xn_ready, GT * (2 * NG + g + 1))
                    sp.dma_start(pairs_v[:, t, 0, :], xn[:, t, :]).then_inc(s_pairs, 16)
                    sp.dma_start(pairs_v[:, t, 1, :], xr[:, t, :]).then_inc(s_pairs, 16)

            store_pairs(0)
            sp.dma_start(w2_sb[:, :, :, :], w2).then_inc(s_w2, 16)
            sp.wait_ge(s_scat, 16 * NBLK)
            for g in range(NG):
                t = slice(GT * g, GT * (g + 1))
                sp.dma_start(xr[:, t, :], x1_v[:, t, :]).then_inc(s_x1[g], 16)
            store_pairs(1)

        @block.gpsimd
        def _(pool):
            steps = Steps(pool, pool_step)
            g_ = nc.gpsimd
            steps.did(g_.memset(ident[:, :], 0.0))
            steps.did(g_.memset(half_pi[:, :], float(np.pi / 2)))
            steps.did(g_.memset(round_c[:, :], ROUND))
            steps.did(g_.memset(head_mask[:, :], 1.0))
            steps.did(g_.memset(before[:, :], 1.0))
            steps.did(g_.memset(ones_b[:, :], 1.0))
            steps.did(g_.memset(first_tile[:, :, :], 1.0))
            steps.did(g_.memset(ones_e[:, :], 1.0))
            steps.did(g_.memset(carry[:, :, :], 0.0))
            steps.did(g_.memset(xT[:, 0:PAD], 0.0))
            steps.did(g_.iota(rev_e[:, :], pattern=[[-1, E]], base=E, channel_multiplier=0, allow_small_or_imprecise_dtypes=True))
            steps.did(g_.iota(blk_no[:, :], pattern=[[1, NBLK]], base=0, channel_multiplier=0, allow_small_or_imprecise_dtypes=True))
            steps.did(g_.iota(tok_no[:, :], pattern=[[0, 1]], base=0, channel_multiplier=1, allow_small_or_imprecise_dtypes=True))
            steps.did(g_.iota(tile_no[:, :], pattern=[[1, NT]], base=1, channel_multiplier=0, allow_small_or_imprecise_dtypes=True))
            steps.did(g_.iota(slot_no[:, :], pattern=[[1, P]], base=0, channel_multiplier=0, allow_small_or_imprecise_dtypes=True))
            steps.did(g_.iota(no_tok[:, :], pattern=[[P, NBLK]], base=L + P, channel_multiplier=1, allow_small_or_imprecise_dtypes=True))
            steps.did(g_.memset(rows[:, :, :, :], 0.0))
            steps.did(g_.iota(head_i[:, :], pattern=[[0, 1]], base=0, channel_multiplier=1))
            steps.did(g_.memset(expand[:, :], 1.0))
            steps.wait()
            steps.did(g_.affine_select(out=ident[:, :], in_=ident[:, :], compare_op=ALU.not_equal, fill=1.0, base=0,
                                       pattern=[[-1, P]], channel_multiplier=1))
            steps.did(g_.affine_select(out=before[:, :], in_=before[:, :], compare_op=ALU.is_ge, fill=0.0, base=-1,
                                       pattern=[[1, P]], channel_multiplier=-1))
            steps.did(g_.memset(first_tile[:, :, 0:1], 0.0))
            steps.then(g_.affine_select(out=head_mask[:, :], in_=head_mask[:, :], compare_op=ALU.is_ge, fill=0.0, base=0,
                                        pattern=[[-H, K]], channel_multiplier=1))
            g_.affine_select(out=head_mask[:, :], in_=head_mask[:, :], compare_op=ALU.is_ge, fill=0.0, base=H - 1,
                             pattern=[[H, K]], channel_multiplier=-1).then_inc(const_ready, 1)
            pool.wait_ge(const_ready, 1)
            for c in range(NG):
                e = expand[K * c:K * (c + 1), :]
                steps.then(g_.iota(pos[K * c:K * (c + 1), :], pattern=[[1, CH]], base=CH * c, channel_multiplier=0, allow_small_or_imprecise_dtypes=True))
                steps.then(g_.affine_select(out=e, in_=e, compare_op=ALU.is_ge, fill=0.0, base=0, pattern=[[1, P]], channel_multiplier=-H))
                steps.then(g_.affine_select(out=e, in_=e, compare_op=ALU.is_ge, fill=0.0, base=H - 1, pattern=[[-1, P]], channel_multiplier=H))
            pool.wait_ge(s_small, N_SMALL)
            g_.tensor_tensor(cw_sb[:, :, :], cw_sb[:, :, :],
                             inw_sb[:, 0:2 * D].rearrange("p (a n) -> p a n", a=1).broadcast_to([P, CK, 2 * D]),
                             ALU.mult).then_inc(wz_ready, 1)
            g_.tensor_scalar(th_sb[:, :], th_sb[:, :], float(1 / (2 * np.pi)), 0.0, ALU.mult, ALU.add).then_inc(th_ready, 1)
            steps.then(g_.tensor_tensor(wri_sb[:, :, :, :], wri_sb[:, :, :, :],
                                        ns_sb[:, :, :].rearrange("p r (m a) -> p r m a", a=1).broadcast_to([P, 2, M, H]), ALU.mult))
            for i in range(2 * M):
                g_.tensor_tensor(wbd_sb[:, i, :, :],
                                 wri_sb[:, i // M, i % M, :].rearrange("p (a h) -> p a h", a=1).broadcast_to([P, K, H]),
                                 head_mask[:, :].rearrange("p (k a) -> p k a", a=1).broadcast_to([P, K, H]),
                                 ALU.mult).then_inc(wbd_ready, 1)

            def token_blocks(f):
                pool.wait_ge(slot_ready, f + 1)
                col = lambda ap: ap.rearrange("p (n a) -> p n a", a=1).broadcast_to([P, NT, NBLK])
                g_.tensor_tensor(in_blk[:, :, 0, :], in_blk[:, :, 2, :], col(tile_no[:, :]), ALU.mult).then_inc(in_blk_ready, 1)
                g_.tensor_scalar(in_blk[:, :, 1, :], in_blk[:, :, 2, :], tok_no[:, 0:1], 0.0, ALU.mult, ALU.add).then_inc(in_blk_ready, 1)

            def blocks(f):
                b0 = NBLK * f
                dst = (x1_rows, out)[f]

                def gather(b):
                    g_.indirect_dma_start(out=rows[:, b % RING, :, :].rearrange("p i d -> p (i d)"), out_offset=None, in_=pairs[:, :],
                                          in_offset=bass.IndirectOffsetOnAxis(ap=tok_i[:, b:b + 1], axis=0),
                                          bounds_check=L - 1, oob_is_err=False).then_inc(s_rows[b % RING], 16)

                def scatter(b):
                    pool.wait_ge(yb_ready, b + b0 + 1)
                    g_.indirect_dma_start(out=dst[:, :], out_offset=bass.IndirectOffsetOnAxis(ap=tok_i[:, b:b + 1], axis=0),
                                          in_=res[:, b, :], in_offset=None,
                                          bounds_check=L - 1, oob_is_err=False).then_inc(s_scat, 16)

                pool.wait_ge(tok_ready, f + 1)
                pool.wait_ge(s_pairs, 16 * 2 * NG * (f + 1))
                for b in range(RING):
                    gather(b)
                for b in range(NBLK):
                    scatter(b)
                    if b + RING < NBLK:
                        gather(b + RING)

            def phases(c):
                x_c = val[:, c % 2, :]
                pool.wait_ge(val_ready, c + 1)
                if c >= 1:
                    pool.wait_ge(cos_ready, c)
                    pool.wait_ge(g_ready, c)
                else:
                    pool.wait_ge(dmix_ready, 1)
                    pool.wait_ge(th_ready, 1)
                for m in range(M):
                    g_.tensor_scalar(ub[:, m, :], x_c, th_sb[:, m:m + 1], 0.0, ALU.mult, ALU.add).then_inc(u_ready, 1)
                steps.then(g_.tensor_scalar(ga, x_c, dmix[:, 6:7], dmix[:, 4:5], ALU.mult, ALU.add))
                g_.tensor_tensor(ga, ga, x_c, ALU.mult).then_inc(poly_ready, 1)

            def imag(c):
                pool.wait_ge(g_ready, c + 1)
                pool.wait_ge(sin_ready, c + 1)
                if c >= 1:
                    pool.wait_ge(im_sums, M * c)
                g_.tensor_tensor(imb[:, :, :], sn[:, :, :],
                                 g_sb.rearrange("p (a n) -> p a n", a=1).broadcast_to([P, M, CH]), ALU.mult).then_inc(im_ready, 1)

            def add_squares(c):
                pool.wait_ge(sq_ready, 3 * (c + 1))
                steps.then(g_.tensor_tensor(sq[:, 0:4, :], sq[:, 0:4, :], sq[:, 4:8, :], ALU.add))
                steps.then(g_.tensor_tensor(sq[:, 0:2, :], sq[:, 0:2, :], sq[:, 2:4, :], ALU.add))
                g_.tensor_tensor(sq[:, 0, :], sq[:, 0, :], sq[:, 1, :], ALU.add).then_inc(sqs_ready, 1)

            token_blocks(0)
            pool.wait_ge(s_b, 32)
            g_.tensor_scalar(b2_sb[:, :, :], b2_sb[:, :, :], 0.5, 0.0, ALU.mult, ALU.add).then_inc(b2_ready, 1)
            blocks(0)
            phases(0)
            imag(0)
            phases(1)
            for c in range(NG):
                add_squares(c)
                if c + 1 < NG:
                    imag(c + 1)
                if c + 2 < NG:
                    phases(c + 2)
            token_blocks(1)
            blocks(1)
            pool.wait_ge(s_scat, 16 * 2 * NBLK)

        @block.scalar
        def _(act):
            steps = Steps(act, act_step)

            def to_free(q):
                g = q % NG
                act.wait_ge(xt_done, q + 1)
                nc.scalar.copy(xT[:, PAD + CH * g:PAD + CH * (g + 1)], p_turned(q)[:, :]).then_inc(xT_ready, 1)

            to_free(0)
            to_free(1)
            act.wait_ge(pre_dve, 1)
            nc.scalar.activation(ln1[:, 1:2], ln1[:, 0:1], ACT.Exp, scale=-1.0).then_inc(pre_act, 1)
            act.wait_ge(pre_dve, 2)
            nc.scalar.activation(dl_sb[:, :], dl_sb[:, :], ACT.Exp).then_inc(pre_act, 1)
            to_free(2)
            to_free(3)
            act.wait_ge(pre_dve, 3)
            nc.scalar.activation(tw[:, :], pos[:, :], ACT.Exp, scale=ln1[:, 0:1]).then_inc(pre_act, 1)

            def blocks(f):
                b0 = NBLK * f

                def copy_x(b, r):
                    act.wait_ge(tx_done, b + b0 + 1)
                    if isinstance(b, int) and r + b0 >= 2:
                        act.wait_ge(h_done, b + b0 - 1)
                    nc.scalar.copy(xsT[:, r % 2, :], p_xs[r % 2][:, 0:P]).then_inc(xsT_ready, 1)

                def relu(b, r):
                    act.wait_ge(th_done, b + b0 + 1)
                    if isinstance(b, int) and r + b0 >= 2:
                        act.wait_ge(y_done, b + b0 - 1)
                    nc.scalar.activation(hT[:, r % 2, :], p_ht[r % 2][:, :], ACT.Relu).then_inc(hT_ready, 1)

                copy_x(0, 0)
                copy_x(1, 1)
                for b in range(LEAD):
                    copy_x(b + 2, b + 2)
                    relu(b, b)
                with act.Fori(0, TURNS) as t:
                    for r in range(LEAD, LEAD + RING):
                        copy_x(t * RING + (r + 2), r + 2)
                        relu(t * RING + r, r)
                for b in range(TAIL, NBLK):
                    if b + 2 < NBLK:
                        copy_x(b + 2, b + 2)
                    relu(b, b)

            def values(c):
                act.wait_ge(zv_done, c + 1)
                if c >= 2:
                    act.wait_ge(poly_ready, c - 1)
                nc.scalar.activation(val[:, c % 2, :], p_a[:, :], ACT.Identity, bias=cbv_sb[:, 0:1]).then_inc(val_ready, 1)

            def score_copy(i):
                h = slice(64 * i, 64 * (i + 1))
                act.wait_ge(s_done, i + 1)
                nc.scalar.copy(zs[h, 0:PAD], p_y[h, 0:PAD]).then_inc(zs_ready, 1)
                nc.scalar.copy(zs[h, PAD:PAD + CH], p_x[h, :]).then_inc(zs_ready, 1)

            def score_exp(i):
                h = slice(64 * i, 64 * (i + 1))
                act.wait_ge(sx_ready, i + 1)
                nc.scalar.activation(sx[h, :], sx[h, :], ACT.Exp).then_inc(ex_ready, 1)

            def gates(c):
                act.wait_ge(zg_done, c + 1)
                nc.scalar.activation(gate[:, c, :], p_b[:, :], ACT.Silu, bias=cbv_sb[:, 1:2]).then_inc(gate_ready, 1)

            def trig(c):
                act.wait_ge(u_ready, M * (c + 1))
                nc.scalar.activation(vb[:, :, :], ub[:, :, :], ACT.Identity, bias=round_c[:, :]).then_inc(v_ready, 1)
                act.wait_ge(r_ready, c + 1)
                nc.scalar.activation(ub[:, :, :], vb[:, :, :], ACT.Abs).then_inc(abs_ready, 1)
                if c >= 1:
                    act.wait_ge(im_ready, c)
                nc.scalar.activation(sn[:, :, :], vb[:, :, :], ACT.Sin, scale=-TWO_PI).then_inc(sin_ready, 1)
                act.wait_ge(abs_ready, c + 1)
                if c >= 1:
                    act.wait_ge(re_sums, M * c)
                nc.scalar.activation(cs[:, :, :], ub[:, :, :], ACT.Sin, scale=-TWO_PI, bias=half_pi[:, :]).then_inc(cos_ready, 1)

            def squares(c):
                if c >= 1:
                    act.wait_ge(sq_done, c)
                act.wait_ge(re_sums, M * (c + 1))
                nc.scalar.activation(sq[:, 0:M, :], num[:, 0:M, :], ACT.Square).then_inc(sq_ready, 1)
                act.wait_ge(dmx_ready, c + 1)
                nc.scalar.activation(sq[:, 2 * M, :], dmx, ACT.Square, scale=float(np.sqrt(EPS / S_DIV / H))).then_inc(sq_ready, 1)
                act.wait_ge(im_sums, M * (c + 1))
                nc.scalar.activation(sq[:, M:2 * M, :], num[:, M:2 * M, :], ACT.Square).then_inc(sq_ready, 1)

            blocks(0)
            to_free(NG)
            to_free(NG + 1)
            values(0)
            score_copy(0)
            score_exp(0)
            gates(0)
            trig(0)
            to_free(NG + 2)
            values(1)
            to_free(NG + 3)
            score_copy(1)
            score_exp(1)
            gates(1)
            for c in range(NG + 2):
                if c < NG:
                    squares(c)
                if c + 1 < NG:
                    trig(c + 1)
                if c + 2 < NG:
                    values(c + 2)
                    gates(c + 2)
                if c >= 2:
                    to_free(2 * NG + c - 2)
            blocks(1)

        @block.tensor
        def _(pe):
            mm = nc.tensor.matmul
            pe.wait_ge(const_ready, 1)

            def turn(q):
                if q >= 2:
                    pe.wait_ge(xT_ready, q if q > NG else q - 1)
                for n in range(GT):
                    pe.wait_ge(xn_ready, GT * q + n + 1)
                    last = nc.tensor.transpose(p_turned(q)[:, P * n:P * (n + 1)], xn[:, GT * (q % NG) + n, :], ident[:, :])
                last.then_inc(xt_done, 1)

            def logits(q):
                g = q % NG
                pe.wait_ge(xT_ready, q + 1)
                if q >= 2 * NG:
                    pe.wait_ge(tok_ready, 1)
                for n in range(GT * g, GT * (g + 1)):
                    last = mm(LOG[:, n, :], xT[:, PAD + P * n:PAD + P * (n + 1)], gw_sb[:, :], start=True, stop=True)
                last.then_inc(lg_done, 1)

            def ranks(f):
                pe.wait_ge(oh_ready, f + 1)
                oh_v = oh[:, :, :].rearrange("p e n -> p (e n)")
                mm(p_m[:, P:2 * P], before[:, :], oh_v, start=True, stop=True)
                mm(p_m[:, 2 * P:3 * P], ones_b[:, :], oh_v, start=True, stop=True).then_inc(rank_done, 1)

            def slot_tokens(f):
                pe.wait_ge(in_blk_ready, 2 * (f + 1))
                for n in range(NT):
                    if n % GT == 0:
                        pe.wait_ge(in_slot_ready, NG * f + n // GT + 1)
                    last = mm(p_c[:, 0:2 * NBLK], in_slot[:, n, :], in_blk[:, n, 0:2, :].rearrange("p i b -> p (i b)"),
                              start=(n == 0), stop=(n == NT - 1))
                last.then_inc(inv_done, 1)

            def blocks(f):
                b0 = NBLK * f

                def turn_x(b, r, t=0):
                    gathers = f * ((NBLK - r % RING + RING - 1) // RING) + r // RING + 1
                    pe.wait_ge(s_rows[r % RING], t * 16 + 16 * gathers)
                    nc.tensor.transpose(p_xs[r % 2][:, 0:P], rows[:, r % RING, 0, :], ident[:, :]).then_inc(tx_done, 1)

                def expert(b):
                    return pe.value_load(exp_i[0:1, bass.ds(b, 1)], min_val=0, max_val=E - 1)

                def hidden(b, r, e):
                    pe.wait_ge(xsT_ready, b + b0 + 1)
                    mm(p_h[r % 2][:, :], xsT[:, r % 2, :], w1_sb[:, bass.ds(e, 1), :].rearrange("p a h -> p (a h)"),
                       start=True, stop=True).then_inc(h_done, 1)

                def turn_h(b, r):
                    pe.wait_ge(hb_ready, b + b0 + 1)
                    for j in range(HC):
                        last = nc.tensor.transpose(p_ht[r % 2][:, P * j:P * (j + 1)], hb[:, r % 2, P * j:P * (j + 1)], ident[:, :])
                    last.then_inc(th_done, 1)

                def expert_out(b, r, e):
                    pe.wait_ge(hT_ready, b + b0 + 1)
                    if r + b0 >= 2:
                        pe.wait_ge(yb_ready, b + b0 - 1)
                    for j in range(HC):
                        last = mm(p_ys[r % 2][:, 0:P], hT[:, r % 2, P * j:P * (j + 1)],
                                  w2_sb[:, bass.ds(e, 1), j, :].rearrange("p a d -> p (a d)"),
                                  start=(j == 0), stop=(j == HC - 1))
                    last.then_inc(y_done, 1)

                pe.wait_ge(ids_ready, f + 1)
                turn_x(0, 0)
                turn_x(1, 1)
                pe.wait_ge(s_w1, 16)
                hidden(0, 0, expert(0))
                pe.wait_ge(s_w2, 16)
                for b in range(LEAD):
                    e_h = expert(b + 1)
                    turn_x(b + 2, b + 2)
                    hidden(b + 1, b + 1, e_h)
                    if b:
                        e_y = expert(b - 1)
                    turn_h(b, b)
                    if b:
                        expert_out(b - 1, b - 1, e_y)
                with pe.Fori(0, TURNS) as t:
                    for r in range(LEAD, LEAD + RING):
                        e_h = expert(t * RING + (r + 1))
                        turn_x(t * RING + (r + 2), r + 2, t)
                        hidden(t * RING + (r + 1), r + 1, e_h)
                        e_y = expert(t * RING + (r - 1))
                        turn_h(t * RING + r, r)
                        expert_out(t * RING + (r - 1), r - 1, e_y)
                for b in range(TAIL, NBLK):
                    if b + 1 < NBLK:
                        e_h = expert(b + 1)
                    if b + 2 < NBLK:
                        turn_x(b + 2, b + 2)
                    if b + 1 < NBLK:
                        hidden(b + 1, b + 1, e_h)
                    e_y = expert(b - 1)
                    turn_h(b, b)
                    expert_out(b - 1, b - 1, e_y)
                expert_out(NBLK - 1, NBLK - 1, expert(NBLK - 1))

            def scores(i):
                if i:
                    pe.wait_ge(zs_ready, 2)
                for c in range(2 * i, 2 * i + 2):
                    mm(p_x[K * c:K * (c + 1), :], inw_sb[:, 2 * D:TOTAL], xT[:, PAD + CH * c:PAD + CH * (c + 1)], start=True, stop=True)
                    last = mm(p_y[K * c:K * (c + 1), 0:PAD], inw_sb[:, 2 * D:TOTAL], xT[:, CH * c:CH * c + PAD], start=True, stop=True)
                last.then_inc(s_done, 1)

            def project_values(c):
                if c >= 1:
                    pe.wait_ge(val_ready, c)
                for j in range(CK):
                    last = mm(p_a[:, :], cw_sb[:, j, 0:D], xT[:, CH * c + j:CH * c + j + CH], start=(j == 0), stop=(j == CK - 1))
                last.then_inc(zv_done, 1)

            def project_gates(c):
                if c >= 1:
                    pe.wait_ge(gate_ready, c)
                for j in range(CK):
                    last = mm(p_b[:, :], cw_sb[:, j, D:2 * D], xT[:, CH * c + j:CH * c + j + CH], start=(j == 0), stop=(j == CK - 1))
                last.then_inc(zg_done, 1)

            def spread(dst, src):
                return nc.tensor.transpose(dst, src.rearrange("p k h -> p (k h)"), ident[:, :])

            def weights(c):
                pe.wait_ge(pw_ready, 1 + c // 2)
                if c >= 1:
                    pe.wait_ge(pwp_used, c)
                rows_c = slice(K * c, K * (c + 1))
                mm(p_c[:, :], expand[rows_c, :], pw[rows_c, :], start=True, stop=True).then_inc(pwp_done, 1)

            def heads(c):
                if c >= 2:
                    pe.wait_ge(yt_ready, c - 1)
                else:
                    pe.wait_ge(zs_ready, 4)
                for i in range(2 * M):
                    if i == 0:
                        pe.wait_ge(re_sums, M * (c + 1))
                    if i == M:
                        pe.wait_ge(im_sums, M * (c + 1))
                    last = mm(p_hd[c % 2][:, :], wbd_sb[:, i, :, :].rearrange("p k h -> p (k h)"), num[:, i, :],
                              start=(i == 0), stop=(i == 2 * M - 1))
                last.then_inc(w_done, 1)

            def square_sums(c):
                pe.wait_ge(sqs_ready, c + 1)
                if c >= 1:
                    pe.wait_ge(rs_ready, c)
                for n in range(GT):
                    for i in (0, 2 * M):
                        last = mm(SQS[:, K * n:K * (n + 1)], sq[:, i, P * n:P * (n + 1)], head_mask[:, :],
                                  start=(i == 0), stop=(i == 2 * M))
                last.then_inc(sq_done, 1)

            def spread_rs(c):
                pe.wait_ge(rs_ready, c + 1)
                if c >= 1:
                    pe.wait_ge(x_ready, c)
                for n in range(GT):
                    last = spread(p_d[:, P * n:P * (n + 1)], rs[:, n, :, :])
                last.then_inc(rsp_done, 1)

            def outputs(c):
                pe.wait_ge(yt_ready, c + 1)
                for n in range(GT):
                    last = mm(p_d[:, P * n:P * (n + 1)], ygt[:, P * n:P * (n + 1)], ow_sb[:, :], start=True, stop=True)
                last.then_inc(o_done, 1)

            pe.wait_ge(s_small, N_SMALL)
            turn(0)
            for q in range(1, NG):
                turn(q)
                logits(q - 1)
            logits(NG - 1)
            ranks(0)
            slot_tokens(0)
            blocks(0)
            turn(NG)
            turn(NG + 1)
            pe.wait_ge(wbd_ready, 2 * M)
            pe.wait_ge(xT_ready, NG + 1)
            project_values(0)
            pe.wait_ge(xT_ready, NG + 2)
            scores(0)
            project_gates(0)
            weights(0)
            turn(NG + 2)
            project_values(1)
            turn(NG + 3)
            pe.wait_ge(xT_ready, 2 * NG)
            scores(1)
            project_gates(1)
            weights(1)
            for c in range(NG + 2):
                if 1 <= c <= NG:
                    square_sums(c - 1)
                if c < NG:
                    heads(c)
                if c + 2 < NG:
                    project_values(c + 2)
                    project_gates(c + 2)
                if 1 <= c <= NG:
                    spread_rs(c - 1)
                if c >= 2:
                    turn(2 * NG + c - 2)
                if 1 <= c <= NG:
                    outputs(c - 1)
                if c + 2 < NG:
                    weights(c + 2)
                if c >= 2:
                    logits(2 * NG + c - 2)
            ranks(1)
            slot_tokens(1)
            blocks(1)

        @block.vector
        def _(dve):
            steps = Steps(dve, dve_step)
            v = nc.vector
            ts, tt, stt = v.tensor_scalar, v.tensor_tensor, v.scalar_tensor_tensor

            def over(ap, n):
                return ap.rearrange("p (a m) -> p a m", a=1).broadcast_to([ap.shape[0], n, ap.shape[1]])

            def each(ap, n):
                return ap.rearrange("p (m a) -> p m a", a=1).broadcast_to([ap.shape[0], ap.shape[1], n])

            def rsqrt(y, a, t):
                steps.then(ts(y.bitcast(I32), a.bitcast(I32), -0.5, RSQRT_SEED, ALU.mult, ALU.add))
                for _ in range(3):
                    steps.then(stt(t, y, -0.5, y, ALU.mult, ALU.mult))
                    steps.then(tt(t, t, a, ALU.mult))
                    steps.then(stt(y, t, 1.5, y, ALU.add, ALU.mult))

            def moments(n0, nt, var, loads=None):
                tiles = slice(0, nt)
                for n in range(nt):
                    if loads and n % GT == 0:
                        dve.wait_ge(loads[(n0 + n) // GT], 16)
                    steps.did(v.bn_stats(st[:, n, :], xr[:, n0 + n, :]))
                steps.wait()
                steps.did(tt(ln[:, 0, tiles], st[:, tiles, 1], st[:, tiles, 4], ALU.subtract))
                steps.did(tt(ln[:, 1, tiles], st[:, tiles, 1], st[:, tiles, 4], ALU.add))
                steps.then(tt(ln[:, 2, tiles], st[:, tiles, 2], st[:, tiles, 5], ALU.add))
                steps.did(stt(ln[:, 3, tiles], ln[:, 0, tiles], 0.25, ln[:, 0, tiles], ALU.mult, ALU.mult))
                steps.did(ts(ln[:, 4, tiles], ln[:, 1, tiles], 0.5, None, ALU.mult))
                steps.then(ts(ln[:, 2, tiles], ln[:, 2, tiles], 1.0 / D, EPS, ALU.mult, ALU.add))
                steps.then(tt(var, ln[:, 2, tiles], ln[:, 3, tiles], ALU.add))

            def normalise(q, n0, nt, rstd):
                if q == NG:
                    dve.wait_ge(xt_done, NG)
                    dve.wait_ge(s_pairs, 16 * 2 * NG)
                if q >= 2 * NG:
                    dve.wait_ge(xt_done, 2 * NG)
                for n in range(nt):
                    ts(xn[:, n0 + n, :], xr[:, n0 + n, :], ln[:, 4, n:n + 1], rstd[:, n:n + 1],
                       ALU.subtract, ALU.mult).then_inc(xn_ready, 1)
                dve.wait_ge(xn_ready, GT * q + nt)

            def norm(q, n0, nt):
                tiles = slice(0, nt)
                moments(n0, nt, ln[:, 5, tiles], loads=s_x if q == 0 else s_x1)
                rsqrt(ln[:, 6, tiles], ln[:, 5, tiles], ln[:, 7, tiles])
                normalise(q, n0, nt, ln[:, 6, :])

            def route(f):
                dve.wait_ge(lg_done, NG * (f + 1))
                by_token = lg[:, :, :].rearrange("p e n -> p n e")
                steps.then(tt(by_token, LOG, over(gb_sb[:, :], NT), ALU.add))
                steps.then(v.tensor_reduce(mx[:, :], by_token, AX.X, ALU.max))
                steps.then(tt(rt[:, 0, :, :], lg[:, :, :], over(mx[:, :], E), ALU.is_equal))
                steps.then(tt(rt[:, 0, :, :], rt[:, 0, :, :], each(rev_e[:, :], NT), ALU.mult))
                steps.then(v.tensor_reduce(mx[:, :], rt[:, 0, :, :].rearrange("p e n -> p n e"), AX.X, ALU.max))
                tt(oh[:, :, :], rt[:, 0, :, :], over(mx[:, :], E), ALU.is_equal).then_inc(oh_ready, 1)
                dve.wait_ge(rank_done, f + 1)
                steps.then(v.tensor_tensor_scan(rt[:, 1, :, :].rearrange("p e n -> p (e n)"),
                                                first_tile[:, :, :].rearrange("p e n -> p (e n)"),
                                                p_m[:, 2 * P:3 * P], 0.0, ALU.mult, ALU.add))
                steps.did(tt(rt[:, 0, :, :], rt[:, 1, :, :], TOT, ALU.subtract))
                steps.then(ts(re8[:, 0, :], rt[:, 1, :, NT - 1], 1.0 / P, 0.5 - 1.0 / (2 * P), ALU.mult, ALU.add))
                steps.did(tt(rt[:, 0, :, :], rt[:, 0, :, :], RANK, ALU.add))
                steps.then(ts(re8[:, 0, :], re8[:, 0, :], ROUND_POS, ROUND_POS, ALU.add, ALU.subtract))
                steps.then(v.tensor_tensor_scan(re8[:, 1, :], ones_e[:, :], re8[:, 0, :], 0.0, ALU.mult, ALU.add))
                steps.did(tt(cmp_b[:, :, :], each(blk_no[0:1, :], E), over(re8[0:1, 1, :], NBLK), ALU.is_ge))
                steps.then(tt(re8[:, 2, :], re8[:, 1, :], re8[:, 0, :], ALU.subtract))
                steps.then(stt(rt[:, 0, :, :], each(re8[:, 2, :], NT), float(P), rt[:, 0, :, :], ALU.mult, ALU.add))
                steps.then(tt(rt[:, 0, :, :], rt[:, 0, :, :], oh[:, :, :], ALU.mult))
                steps.then(v.tensor_reduce(mx[:, :], rt[:, 0, :, :].rearrange("p e n -> p n e"), AX.X, ALU.add))
                steps.then(ts(slot_b[:, 0, :], mx[:, :], 1.0 / P, 1.0 / (2 * P) - 0.5, ALU.mult, ALU.add))
                steps.then(ts(slot_b[:, 0, :], slot_b[:, 0, :], ROUND, ROUND, ALU.add, ALU.subtract))
                steps.did(stt(slot_b[:, 1, :], slot_b[:, 0, :], -float(P), mx[:, :], ALU.mult, ALU.add))
                tt(in_blk[:, :, 2, :], each(slot_b[:, 0, :], NBLK), over(blk_no[:, :], NT), ALU.is_equal).then_inc(slot_ready, 1)
                steps.wait()
                for n in range(0, NT, GT):
                    tt(in_slot[:, n:n + GT, :], each(slot_b[:, 1, n:n + GT], P), over(slot_no[:, :], GT), ALU.is_equal).then_inc(in_slot_ready, 1)
                steps.then(v.tensor_reduce(exp_f[:, :], cmp_b[:, :, :], AX.X, ALU.add))
                ts(exp_i[:, :], exp_f[:, :], float(E - 1), None, ALU.min).then_inc(ids_ready, 1)
                dve.wait_ge(inv_done, f + 1)
                steps.then(ts(inv[:, 0, :], INV[:, 0, :], 0.0, None, ALU.is_equal))
                steps.then(tt(inv[:, 0, :], inv[:, 0, :], no_tok[:, :], ALU.mult))
                steps.then(stt(inv[:, 0, :], INV[:, 0, :], float(P), inv[:, 0, :], ALU.mult, ALU.add))
                stt(tok_i[:, :], inv[:, 0, :], -float(P), INV[:, 1, :], ALU.add, ALU.add).then_inc(tok_ready, 1)
                dve.wait_ge(ids_ready, f + 1)
                dve.wait_ge(tok_ready, f + 1)

            def blocks(f):
                b0 = NBLK * f

                def add_b1(b, r):
                    e = dve.value_load(exp_i[0:1, bass.ds(b, 1)], min_val=0, max_val=E - 1)
                    dve.wait_ge(h_done, b + b0 + 1)
                    if isinstance(b, int) and r + b0 >= 2:
                        dve.wait_ge(th_done, b + b0 - 1)
                    tt(hb[:, r % 2, :], p_h[r % 2][:, :], b1_sb[:, bass.ds(e, 1), :].rearrange("p a h -> p (a h)"),
                       ALU.add).then_inc(hb_ready, 1)

                def add_x(b, r):
                    e = dve.value_load(exp_i[0:1, bass.ds(b, 1)], min_val=0, max_val=E - 1)
                    tt(rows[:, r % RING, 1, :], rows[:, r % RING, 1, :],
                       b2_sb[:, bass.ds(e, 1), :].rearrange("p a d -> p (a d)"), ALU.add).then_inc(xb_ready, 1)

                def sums(b, r):
                    dve.wait_ge(y_done, b + b0 + 1)
                    dve.wait_ge(xb_ready, b + b0 + 1)
                    stt(res[:, bass.ds(b, 1), :].rearrange("p a d -> p (a d)"), p_ys[r % 2][:, 0:P], 0.5,
                        rows[:, r % RING, 1, :], ALU.mult, ALU.add).then_inc(yb_ready, 1)

                if f == 0:
                    dve.wait_ge(s_b, 32)
                    dve.wait_ge(b2_ready, 1)
                add_b1(0, 0)
                for b in range(LEAD):
                    add_b1(b + 1, b + 1)
                    add_x(b, b)
                    if b:
                        sums(b - 1, b - 1)
                with dve.Fori(0, TURNS) as t:
                    for r in range(LEAD, LEAD + RING):
                        add_b1(t * RING + (r + 1), r + 1)
                        add_x(t * RING + r, r)
                        sums(t * RING + (r - 1), r - 1)
                for b in range(TAIL, NBLK):
                    if b + 1 < NBLK:
                        add_b1(b + 1, b + 1)
                    add_x(b, b)
                    sums(b - 1, b - 1)
                sums(NBLK - 1, NBLK - 1)

            def prelude():
                dve.wait_ge(s_small, N_SMALL)
                dve.wait_ge(wbd_ready, 2 * M)
                slope = sp_sb[:, CK + 2:CK + 3]
                ts(ln1[:, 0:1].bitcast(I32), slope.bitcast(I32), 0x7FFFFFFF, None, ALU.bitwise_and).then_inc(pre_dve, 1)
                steps.then(v.tensor_reduce(dmix[:, 0:1], dl_sb[:, :], AX.X, ALU.max))
                ts(dl_sb[:, :], dl_sb[:, :], dmix[:, 0:1], None, ALU.subtract).then_inc(pre_dve, 1)
                steps.then(ts(head_i[:, :], head_i[:, :], K - 1, None, ALU.bitwise_and))
                steps.then(ts(anchor[:, 0:1], head_i[:, :], float(K - A), None, ALU.is_ge))
                steps.did(ts(anchor[:, 1:2], anchor[:, 0:1], 2.0, -1.0, ALU.mult, ALU.add))
                steps.then(ts(anchor[:, 2:3], anchor[:, 0:1], -float(L - 1), float(L - 1), ALU.mult, ALU.add))
                steps.did(ts(pos[:, :], pos[:, :], anchor[:, 1:2], anchor[:, 2:3], ALU.mult, ALU.add))
                dve.wait_ge(pre_act, 1)
                steps.then(ts(ln1[:, 2:3], ln1[:, 1:2], 2.0, None, ALU.add))
                steps.then(v.reciprocal(ln1[:, 2:3], ln1[:, 2:3]))
                steps.then(tt(ln1[:, 1:2], ln1[:, 1:2], ln1[:, 2:3], ALU.mult))
                steps.then(tt(ln1[:, 2:3], ln1[:, 1:2], ln1[:, 1:2], ALU.mult))
                steps.then(ts(ln1[:, 3:4], ln1[:, 2:3], 1.0 / 15, None, ALU.mult))
                for n in range(13, 1, -2):
                    steps.then(stt(ln1[:, 3:4], ln1[:, 3:4], 1.0 / n, ln1[:, 2:3], ALU.add, ALU.mult))
                steps.then(stt(ln1[:, 3:4], ln1[:, 3:4], 1.0, ln1[:, 1:2], ALU.add, ALU.mult))
                steps.then(ts(ln1[:, 4:5], slope, 0.0, None, ALU.max))
                stt(ln1[:, 0:1], ln1[:, 3:4], -2.0, ln1[:, 4:5], ALU.mult, ALU.subtract).then_inc(pre_dve, 1)
                dve.wait_ge(pre_act, 2)
                steps.then(v.tensor_reduce(dmix[:, 1:2], dl_sb[:, :], AX.X, ALU.add))
                steps.then(v.reciprocal(dmix[:, 2:3], dmix[:, 1:2]))
                steps.then(ts(dmix[:, 3:6], dl_sb[:, :], dmix[:, 2:3], None, ALU.mult))
                ts(dmix[:, 6:7], dmix[:, 5:6], -1.0, None, ALU.mult).then_inc(dmix_ready, 1)
                dve.wait_ge(dmix_ready, 1)

            def score_weights(i):
                h = slice(64 * i, 64 * (i + 1))
                tap = lambda j: sp_sb[h, j:j + 1]
                dve.wait_ge(zs_ready, 2 * (i + 1))
                steps.then(ts(sx[h, :], zs[h, PAD:PAD + CH], tap(CK - 1), sp_sb[h, CK:CK + 1], ALU.mult, ALU.add))
                for j in range(CK - 1):
                    steps.then(stt(sx[h, :], zs[h, j:j + CH], tap(j), sx[h, :], ALU.mult, ALU.add))
                steps.then(ts(sx[h, :], sx[h, :], sp_sb[h, CK + 1:CK + 2], -20.0, ALU.mult, ALU.max))
                ts(sx[h, :], sx[h, :], 20.0, None, ALU.min).then_inc(sx_ready, 1)

            def time_weights(i):
                h = slice(64 * i, 64 * (i + 1))
                dve.wait_ge(ex_ready, i + 1)
                dve.wait_ge(pre_act, 3)
                tt(pw[h, :], sx[h, :], tw[h, :], ALU.mult).then_inc(pw_ready, 1)

            def reduce_phase(c):
                dve.wait_ge(v_ready, c + 1)
                stt(vb[:, :, :], vb[:, :, :], ROUND, ub[:, :, :], ALU.subtract, ALU.subtract).then_inc(r_ready, 1)

            def envelope(c):
                dve.wait_ge(poly_ready, c + 1)
                dve.wait_ge(pwp_done, c + 1)
                if c >= 1:
                    dve.wait_ge(im_ready, c)
                stt(g_sb, ga, dmix[:, 3:4], p_c[:, :], ALU.add, ALU.mult).then_inc(g_ready, 1)
                if c >= 1:
                    dve.wait_ge(dmx_ready, c)
                v.tensor_tensor_scan(num[:, 2 * M, :], p_c[:, :], tw[:, :], carry[:, 2 * M, :], ALU.add, ALU.bypass).then_inc(pwp_used, 1)
                dve.wait_ge(pwp_used, c + 1)
                steps.then(v.tensor_copy(carry[:, 2 * M, :], num[:, 2 * M, CH - 1:CH]))
                if c >= 1:
                    dve.wait_ge(sq_ready, 3 * c)
                ts(dmx, num[:, 2 * M, :], 1e-4, None, ALU.max).then_inc(dmx_ready, 1)

            def running_sums(c):
                dve.wait_ge(cos_ready, c + 1)
                dve.wait_ge(g_ready, c + 1)
                tt(cs[:, :, :], cs[:, :, :], over(g_sb, M), ALU.mult).then_inc(re_ready, 1)
                dve.wait_ge(re_ready, c + 1)
                if c >= 1:
                    dve.wait_ge(sq_ready, 3 * c)
                    dve.wait_ge(w_done, c)
                for m in range(M):
                    v.tensor_tensor_scan(num[:, m, :], cs[:, m, :], cs[:, m, :], carry[:, m, :], ALU.add, ALU.bypass).then_inc(re_sums, 1)
                dve.wait_ge(im_ready, c + 1)
                for m in range(M):
                    v.tensor_tensor_scan(num[:, M + m, :], imb[:, m, :], imb[:, m, :], carry[:, M + m, :], ALU.add, ALU.bypass).then_inc(im_sums, 1)
                dve.wait_ge(re_sums, M * (c + 1))
                dve.wait_ge(im_sums, M * (c + 1))
                steps.then(v.tensor_copy(carry[:, 0:2 * M, :], num[:, 0:2 * M, CH - 1:CH]))

            def tail(c_rs, c_ln):
                if c_ln is not None:
                    dve.wait_ge(o_done, c_ln + 1)
                    t = slice(GT * c_ln, GT * (c_ln + 1))
                    tt(xr[:, t, :], xr[:, t, :], p_d[:, :].rearrange("p (n d) -> p n d", d=D), ALU.add).then_inc(x_ready, 1)
                    dve.wait_ge(x_ready, c_ln + 1)
                    moments(GT * c_ln, GT, nw[:, 0, P:P + GT])
                if c_rs is not None:
                    dve.wait_ge(sq_done, c_rs + 1)
                    steps.then(ts(nw[:, 0, 0:P], SQS, S_DIV, None, ALU.mult))
                used = slice(0 if c_rs is not None else P, P + GT if c_ln is not None else P)
                rsqrt(nw[:, 1, used], nw[:, 0, used], nw[:, 2, used])
                if c_rs is not None:
                    if c_rs >= 1:
                        dve.wait_ge(rsp_done, c_rs)
                    v.tensor_copy(rs[:, :, :, :].rearrange("p n k h -> p (n k) h"), each(nw[:, 1, 0:P], H)).then_inc(rs_ready, 1)
                if c_ln is not None:
                    normalise(2 * NG + c_ln, GT * c_ln, GT, nw[:, 1, P:P + GT])

            def gated(c):
                dve.wait_ge(rsp_done, c + 1)
                dve.wait_ge(gate_ready, c + 1)
                if c >= 1:
                    dve.wait_ge(o_done, c)
                steps.then(tt(ygt, gate[:, c, :], p_d[:, :], ALU.mult))
                dve.wait_ge(w_done, c + 1)
                tt(ygt, ygt, p_hd[c % 2][:, :], ALU.mult).then_inc(yt_ready, 1)

            norm(0, 0, NT)
            prelude()
            route(0)
            blocks(0)
            for g in range(NG):
                norm(NG + g, GT * g, GT)
                if g == 1:
                    score_weights(0)
                    reduce_phase(0)
                    time_weights(0)
                    envelope(0)
            score_weights(1)
            time_weights(1)
            for c in range(NG + 2):
                if c < NG:
                    running_sums(c)
                if c + 1 < NG:
                    reduce_phase(c + 1)
                    envelope(c + 1)
                if c >= 1:
                    tail(c - 1 if c <= NG else None, c - 2 if c >= 2 else None)
                if 1 <= c <= NG:
                    gated(c - 1)
            route(1)
            blocks(1)


def kernel(**inputs):
    import concourse.bacc as _bacc
    from concourse.bass_utils import run_bass_kernel_spmd as _run

    a = {k.removeprefix("L0_"): np.asarray(v) for k, v in inputs.items()}
    wri = np.stack([a["attn_W_re"].reshape(H, M, H), a["attn_W_im"].reshape(H, M, H)], axis=1)
    slopes = np.concatenate([a["attn_decay_slopes"], a["attn_anchor_slopes"]])
    ns = a["attn_norm_scale"].reshape(2, H, M).transpose(1, 0, 2)
    heads = np.concatenate([a["attn_conv_w"].reshape(CK, TOTAL)[:, 2 * D:], a["attn_conv_b"][None, 2 * D:],
                            a["attn_score_scale"][None], slopes[None]]).T
    arrays = {
        "x": a["attn_x"].reshape(L, D),
        "gate_w": a["ffn_gate_w"].T,
        "gate_b": a["ffn_gate_b"].reshape(1, E),
        "w1": a["ffn_w1"].transpose(2, 0, 1),
        "b1": a["ffn_b1"].reshape(1, E * HID),
        "w2": a["ffn_w2"].reshape(E, D, HC, P).transpose(3, 0, 2, 1),
        "b2": a["ffn_b2"].reshape(1, E * D),
        "in_w": a["attn_in_proj_w"],
        "conv_w": a["attn_conv_w"].reshape(CK, TOTAL)[:, :2 * D].reshape(1, CK * 2 * D),
        "conv_b": a["attn_conv_b"].reshape(1, TOTAL),
        "theta": a["attn_theta"].reshape(K * H, M),
        "score_par": np.broadcast_to(heads, (NG, K, CK + 3)).reshape(P, CK + 3),
        "deriv": a["attn_deriv_logits"].reshape(1, 3),
        "norm_scale": np.broadcast_to(ns, (K, H, 2, M)).reshape(P, 2, M),
        "w_reim": np.broadcast_to(wri, (K, H, 2, M, H)).reshape(P, 2, M, H),
        "out_w": a["attn_out_proj_w"],
    }
    arrays = {k: np.ascontiguousarray(v) for k, v in arrays.items()}
    nc = _bacc.Bacc("TRN2", target_bir_lowering=False, num_devices=1)
    args = [nc.dram_tensor(f"in_{k}", v.shape, mybir.dt.from_np(v.dtype), kind="ExternalInput").ap()
            for k, v in arrays.items()]
    out = nc.dram_tensor("out_x", (L, D), F32, kind="ExternalOutput").ap()
    build(nc, *args, out)
    r = _run(nc, [{f"in_{k}": v for k, v in arrays.items()}], core_ids=[0])
    return r.results[0]["out_x"].reshape(1, L, D)
```

```python
from contextlib import ExitStack

import numpy as np
import concourse.bass as bass
from concourse import mybir

F32 = mybir.dt.float32
BF16 = mybir.dt.bfloat16
I32 = mybir.dt.int32
ALU = mybir.AluOpType
ACT = mybir.ActivationFunctionType
AX = mybir.AxisListType

P = 128
L = 2048
D = 128
NT = L // P
GT = 4
NG = NT // GT
CH = GT * P
E = 8
HID = 512
HC = HID // P
NBLK = NT + E - 1
RING = 6
LEAD = 3
TURNS = (NBLK - LEAD) // RING
TAIL = LEAD + TURNS * RING
K = 32
H = D // K
M = 4
ACT_M = (2, 0, 0, 2)
A = 4
CK = 4
PAD = CK - 1
TOTAL = 2 * D + K
V_TILES = (3, 2, 3, 2)
EPS = 1e-5
ROUND = 12582912.0
ROUND_POS = 8388608.0
TWO_PI = float(np.nextafter(np.float32(2 * np.pi), np.float32(0)))
RSQRT_SEED = float(0x5F3759DF)
S_DIV = 1.0 / (2.0 * H * M)


class Steps:

    def __init__(self, engine, semaphore):
        self.engine, self.semaphore, self.count = engine, semaphore, 0

    def did(self, instruction):
        self.count += 1
        instruction.then_inc(self.semaphore, 1)

    def wait(self):
        self.engine.wait_ge(self.semaphore, self.count)

    def then(self, instruction):
        self.did(instruction)
        self.wait()


def build(nc, x, gate_w, gate_b, w1, b1, w2, b2, in_w, conv_w, conv_b, theta, score_par, deriv,
          norm_scale, w_reim, out_w, out):
    with ExitStack() as ctx:
        def sb(name, shape, dt=F32):
            return ctx.enter_context(nc.sbuf_tensor(name, shape, dt))

        def pb(name, shape=(P, 512), dt=F32):
            return ctx.enter_context(nc.psum_tensor(name, list(shape), dt))

        def sem(name):
            return ctx.enter_context(nc.semaphore(name))

        pairs = nc.dram_tensor("pairs", (L, 2 * D), F32, kind="Internal").ap()
        x1_rows = nc.dram_tensor("x1_rows", (L, D), F32, kind="Internal").ap()
        pairs_v = pairs.rearrange("(n p) (i d) -> p n i d", p=P, i=2)

        w1_sb = sb("w1_sb", [P, E, HID])
        w2_sb = sb("w2_sb", [P, E, HC, D])
        b1_sb = sb("b1_sb", [P, E, HC])
        b2_sb = sb("b2_sb", [P, E, D])
        gw_sb = sb("gw_sb", [P, E])
        gb_sb = sb("gb_sb", [P, E])
        inw_sb = sb("inw_sb", [P, TOTAL])
        cw_sb = sb("cw_sb", [P, CK, 2 * D])
        cbv_sb = sb("cbv_sb", [P, 2])
        th_sb = sb("th_sb", [P, M])
        sp_sb = sb("sp_sb", [P, CK + 3])
        dl_sb = sb("dl_sb", [P, 3])
        dmix = sb("dmix", [P, 8])
        ns_sb = sb("ns_sb", [P, 2, M])
        wri_sb = sb("wri_sb", [P, 2, M, H])
        wbd_sb = sb("wbd_sb", [P, 2 * M, K, H])
        ow_sb = sb("ow_sb", [P, D])
        ident = sb("ident", [P, P])
        head_mask = sb("head_mask", [P, K])
        before = sb("before", [P, P], BF16)
        ones_b = sb("ones_b", [P, P], BF16)
        first_tile = sb("first_tile", [P, E, NT])
        rev_e = sb("rev_e", [P, E])
        ones_e = sb("ones_e", [P, E])
        blk_no = sb("blk_no", [P, NBLK])
        tok_no = sb("tok_no", [P, 1])
        tile_no = sb("tile_no", [P, NT])
        slot_no = sb("slot_no", [P, P, NT], BF16)
        no_tok = sb("no_tok", [P, NBLK])
        half_pi = sb("half_pi", [P, 1])
        round_c = sb("round_c", [P, 1])
        expand = sb("expand", [P, P])
        tw = sb("tw", [P, CH])
        anchor = sb("anchor", [P, 4])
        head_i = sb("head_i", [P, 1], I32)
        xr = sb("xr", [P, NT, D])
        xn = sb("xn", [P, NT, D])
        rows = sb("rows", [P, RING, 2, D])
        res = sb("res", [P, NBLK, D])
        st = sb("st", [P, NT, 6])
        ln = sb("ln", [P, 8, NT])
        lg = sb("lg", [P, E, NT])
        oh = sb("oh", [P, E, NT], BF16)
        rt = sb("rt", [P, 2, E, NT])
        re8 = sb("re8", [P, 4, E])
        mx = sb("mx", [P, NT])
        slot_b = sb("slot_b", [P, NT])
        slot_s = sb("slot_s", [P, NT], BF16)
        inv = sb("inv", [P, 2, NBLK])
        tok_i = sb("tok_i", [P, NBLK], I32)
        cmp_b = sb("cmp_b", [1, NBLK, E])
        exp_f = sb("exp_f", [1, NBLK])
        exp_i = sb("exp_i", [1, NBLK], I32)
        xT = sb("xT", [P, PAD + L])
        xsT = sb("xsT", [P, 2, P])
        w1_now = sb("w1_now", [P, 2, HID])
        hT = sb("hT", [P, 2, HID])
        zs = sb("zs", [P, PAD + CH])
        sx = sb("sx", [P, CH])
        pw = sx
        val = sb("val", [P, 2, CH])
        gate = sb("gate", [P, NG, CH])
        in_blk = val[:, :, :].rearrange("p i n -> p (i n)").bitcast(BF16)[:, 0:NT * 3 * NBLK].rearrange(
            "p (n i b) -> p n i b", i=3, b=NBLK)
        ub = sb("ub", [P, M, CH])
        vb = sb("vb", [P, M, CH])
        sn = res[:, 0:NT, :].rearrange("p n d -> p (n d)").rearrange("p (m t) -> p m t", m=M)
        cs = sb("cs", [P, 2, M, CH])
        pos = hT[:, 0, :]
        ga = sb("ga", [P, 2, CH])
        g_sb = w1_now[:, 1, :]
        den = sb("den", [P, CH])
        earlier = sb("earlier", [P, P])
        ygt = hT[:, 1, :]
        imb = sb("imb", [P, M, CH])
        num = sb("num", [P, 2 * M, CH])
        carry = sb("carry", [P, 2 * M, 1])
        sq = sb("sq", [P, 2 * M, CH])
        nw = sb("nw", [P, 3, P + 2 * GT])
        rs = rows[:, 0:2, :, :].rearrange("p r i (k h) -> p (r i) k h", h=H)
        ln1 = sb("ln1", [P, 5])

        p_t = pb("p_t")
        p_m = pb("p_m")
        p_a = pb("p_a")
        p_b = pb("p_b")
        p_c = pb("p_c")
        p_d = pb("p_d")
        p_y = pb("p_y")
        p_x = pb("p_x")
        in_slot = w1_now[:, :, :].rearrange("p i n -> p (i n)").bitcast(BF16).rearrange("p (s n) -> p s n", n=NT)
        INV = p_c[:, 0:2 * NBLK].rearrange("p (i b) -> p i b", b=NBLK)
        p_h = (p_a, p_b)
        p_xs, p_ys = (p_x, p_t), (p_y, p_m)
        p_hd = (p_y, p_x)
        p_rs = (p_d, p_d, p_d, p_c)
        squares_of = lambda c: (ub, vb) if c == NG - 1 else (sq[:, 0:M, :], sq[:, M:2 * M, :])
        p_turned = lambda q: (p_t, p_d, p_c, p_b)[q % NG] if q < 2 * NG or q == 3 * NG - 1 else p_t
        LOG = p_a[:, 0:P].rearrange("p (n e) -> p n e", e=E)
        RANK = p_m[:, P:2 * P].rearrange("p (e n) -> p e n", e=E)
        TOT = p_m[:, 2 * P:3 * P].rearrange("p (e n) -> p e n", e=E)
        BEFORE = p_m[:, 0:1]
        SQS = p_m[:, 3 * P:4 * P]

        s_x = [sem(f"s_x{g}") for g in range(NG)]
        s_small = sem("s_small")
        s_w1 = sem("s_w1")
        s_w2 = sem("s_w2")
        s_b = sem("s_b")
        s_pairs = sem("s_pairs")
        s_x1 = [sem(f"s_x1{g}") for g in range(NG)]
        s_rows = [sem(f"s_rows{i}") for i in range(RING)]
        s_scat = sem("s_scat")
        const_ready = sem("const_ready")
        pos_ready = sem("pos_ready")
        wz_ready = sem("wz_ready")
        wbd_ready = sem("wbd_ready")
        th_ready = sem("th_ready")
        pre_dve = sem("pre_dve")
        pre_act = sem("pre_act")
        xn_ready = sem("xn_ready")
        xna_ready = sem("xna_ready")
        rstd_ready = sem("rstd_ready")
        xt_done = sem("xt_done")
        xT_ready = sem("xT_ready")
        xTv_ready = sem("xTv_ready")
        lg_done = sem("lg_done")
        oh_ready = sem("oh_ready")
        rank_done = sem("rank_done")
        slot_ready = sem("slot_ready")
        in_blk_ready = sem("in_blk_ready")
        in_slot_ready = sem("in_slot_ready")
        inv_done = sem("inv_done")
        tok_ready = sem("tok_ready")
        b2_ready = sem("b2_ready")
        ids_ready = sem("ids_ready")
        tx_done = sem("tx_done")
        xsT_ready = sem("xsT_ready")
        h_done = sem("h_done")
        w1_ready = sem("w1_ready")
        hT_ready = sem("hT_ready")
        y_done = sem("y_done")
        xb_ready = sem("xb_ready")
        yb_ready = sem("yb_ready")
        x_ready = sem("x_ready")
        zs_ready = sem("zs_ready")
        dmix_ready = sem("dmix_ready")
        s_done = sem("s_done")
        sx_ready = sem("sx_ready")
        ex_ready = sem("ex_ready")
        pw_ready = sem("pw_ready")
        zv_done = sem("zv_done")
        zg_done = sem("zg_done")
        pwp_done = sem("pwp_done")
        val_ready = sem("val_ready")
        gate_ready = sem("gate_ready")
        u_ready = sem("u_ready")
        ua_ready = sem("ua_ready")
        v_ready = sem("v_ready")
        poly_ready = sem("poly_ready")
        sqs_ready = sem("sqs_ready")
        r_ready = sem("r_ready")
        abs_ready = sem("abs_ready")
        sin_ready = sem("sin_ready")
        cos_ready = sem("cos_ready")
        g_ready = sem("g_ready")
        im_ready = sem("im_ready")
        re_ready = sem("re_ready")
        re_sums = sem("re_sums")
        im_sums = sem("im_sums")
        sums_ready = sem("sums_ready")
        before_done = sem("before_done")
        den_ready = sem("den_ready")
        den2_ready = sem("den2_ready")
        sq_ready = sem("sq_ready")
        w_done = sem("w_done")
        sq_done = sem("sq_done")
        root_ready = sem("root_ready")
        rs_ready = sem("rs_ready")
        rsp_done = sem("rsp_done")
        yt_ready = sem("yt_ready")
        o_done = sem("o_done")
        dve_step = sem("dve_step")
        pool_step = sem("pool_step")
        N_SMALL = 12 * 16

        def xn_waits(engine, q, n):
            f, g = divmod(q, NG)
            if f < 2:
                by_v = sum(V_TILES) * f + sum(V_TILES[:g])
                engine.wait_ge(xn_ready, by_v + min(n + 1, V_TILES[g]))
                if n >= V_TILES[g]:
                    engine.wait_ge(xna_ready, GT * q - by_v + n + 1 - V_TILES[g])
            elif g == NG - 1:
                engine.wait_ge(xn_ready, 2 * sum(V_TILES) + n + 1)
            else:
                engine.wait_ge(xna_ready, 2 * (NT - sum(V_TILES)) + GT * g + n + 1)

        block = ctx.enter_context(nc.Block())

        @block.sync
        def _(sp):
            x_v = x.rearrange("(n p) d -> p n d", p=P)
            x1_v = x1_rows.rearrange("(n p) d -> p n d", p=P)
            for g in range(NG):
                sp.dma_start(xr[:, GT * g:GT * (g + 1), :], x_v[:, GT * g:GT * (g + 1), :]).then_inc(s_x[g], 16)
            for dst, src in ((gw_sb[:, :], gate_w), (gb_sb[:, :], gate_b.broadcast_to([P, E])),
                             (inw_sb[:, :], in_w),
                             (cw_sb[:, :, :].rearrange("p a b -> p (a b)"), conv_w.broadcast_to([P, CK * 2 * D])),
                             (cbv_sb[:, 0:1], conv_b[:, 0:D].rearrange("a p -> p a")),
                             (cbv_sb[:, 1:2], conv_b[:, D:2 * D].rearrange("a p -> p a")),
                             (th_sb[:, :], theta), (sp_sb[:, :], score_par),
                             (dl_sb[:, :], deriv.broadcast_to([P, 3])),
                             (ns_sb[:, :, :], norm_scale), (wri_sb[:, :, :, :], w_reim),
                             (ow_sb[:, :], out_w)):
                sp.dma_start(dst, src).then_inc(s_small, 16)
            sp.dma_start(w1_sb[:, :, :], w1).then_inc(s_w1, 16)
            sp.dma_start(b1_sb[:, :, :], b1).then_inc(s_b, 16)
            sp.dma_start(b2_sb[:, :, :].rearrange("p e d -> p (e d)"), b2.broadcast_to([P, E * D])).then_inc(s_b, 16)

            def store_pairs(f):
                for g in range(NG):
                    t = slice(GT * g, GT * (g + 1))
                    if f == 0:
                        sp.wait_ge(s_x[g], 16)
                        xn_waits(sp, g, GT - 1)
                    else:
                        sp.wait_ge(x_ready, g + 1)
                        xn_waits(sp, 2 * NG + g, GT - 1)
                    sp.dma_start(pairs_v[:, t, 0, :], xn[:, t, :]).then_inc(s_pairs, 16)
                    sp.dma_start(pairs_v[:, t, 1, :], xr[:, t, :]).then_inc(s_pairs, 16)

            store_pairs(0)
            sp.dma_start(w2_sb[:, :, :, :], w2).then_inc(s_w2, 16)
            sp.wait_ge(s_scat, 16 * NBLK)
            for g in range(NG):
                t = slice(GT * g, GT * (g + 1))
                sp.dma_start(xr[:, t, :], x1_v[:, t, :]).then_inc(s_x1[g], 16)
            store_pairs(1)

        @block.gpsimd
        def _(pool):
            steps = Steps(pool, pool_step)
            g_ = nc.gpsimd
            steps.did(g_.memset(ident[:, :], 0.0))
            steps.did(g_.memset(half_pi[:, :], float(np.pi / 2)))
            steps.did(g_.memset(round_c[:, :], ROUND))
            steps.did(g_.memset(head_mask[:, :], 1.0))
            steps.did(g_.memset(before[:, :], 1.0))
            steps.did(g_.memset(ones_b[:, :], 1.0))
            steps.did(g_.memset(first_tile[:, :, :], 1.0))
            steps.did(g_.memset(ones_e[:, :], 1.0))
            steps.did(g_.memset(carry[:, :, :], 0.0))
            steps.did(g_.memset(xT[:, 0:PAD], 0.0))
            steps.did(g_.iota(rev_e[:, :], pattern=[[-1, E]], base=E, channel_multiplier=0, allow_small_or_imprecise_dtypes=True))
            steps.did(g_.iota(blk_no[:, :], pattern=[[1, NBLK]], base=0, channel_multiplier=0, allow_small_or_imprecise_dtypes=True))
            steps.did(g_.iota(tok_no[:, :], pattern=[[0, 1]], base=0, channel_multiplier=1, allow_small_or_imprecise_dtypes=True))
            steps.did(g_.iota(tile_no[:, :], pattern=[[1, NT]], base=1, channel_multiplier=0, allow_small_or_imprecise_dtypes=True))
            steps.did(g_.iota(no_tok[:, :], pattern=[[P, NBLK]], base=L + P, channel_multiplier=1, allow_small_or_imprecise_dtypes=True))
            steps.did(g_.iota(head_i[:, :], pattern=[[0, 1]], base=0, channel_multiplier=1))
            steps.did(g_.memset(expand[:, :], 1.0))
            steps.did(g_.memset(earlier[:, :], 0.0))
            steps.wait()
            steps.did(g_.affine_select(out=ident[:, :], in_=ident[:, :], compare_op=ALU.not_equal, fill=1.0, base=0,
                                       pattern=[[-1, P]], channel_multiplier=1))
            steps.did(g_.affine_select(out=before[:, :], in_=before[:, :], compare_op=ALU.is_ge, fill=0.0, base=-1,
                                       pattern=[[1, P]], channel_multiplier=-1))
            steps.did(g_.memset(first_tile[:, :, 0:1], 0.0))
            steps.then(g_.affine_select(out=head_mask[:, :], in_=head_mask[:, :], compare_op=ALU.is_ge, fill=0.0, base=0,
                                        pattern=[[-H, K]], channel_multiplier=1))
            g_.affine_select(out=head_mask[:, :], in_=head_mask[:, :], compare_op=ALU.is_ge, fill=0.0, base=H - 1,
                             pattern=[[H, K]], channel_multiplier=-1).then_inc(const_ready, 1)
            pool.wait_ge(const_ready, 1)
            for c in range(NG):
                g_.iota(pos[K * c:K * (c + 1), :], pattern=[[1, CH]], base=CH * c, channel_multiplier=0, allow_small_or_imprecise_dtypes=True).then_inc(pos_ready, 1)
                pool.wait_ge(pos_ready, c + 1)
            steps.did(g_.iota(slot_no[:, :, :], pattern=[[1, P], [0, NT]], base=0, channel_multiplier=0, allow_small_or_imprecise_dtypes=True))
            steps.did(g_.memset(rows[:, :, :, :], 0.0))
            for c in range(1, NG):
                steps.then(g_.affine_select(out=earlier[:, :], in_=earlier[:, :], compare_op=ALU.not_equal, fill=1.0, base=K * c,
                                            pattern=[[-1, P]], channel_multiplier=1))
            for c in range(NG):
                e = expand[K * c:K * (c + 1), :]
                steps.then(g_.affine_select(out=e, in_=e, compare_op=ALU.is_ge, fill=0.0, base=0, pattern=[[1, P]], channel_multiplier=-H))
                steps.then(g_.affine_select(out=e, in_=e, compare_op=ALU.is_ge, fill=0.0, base=H - 1, pattern=[[-1, P]], channel_multiplier=H))
            pool.wait_ge(s_small, N_SMALL)
            g_.tensor_tensor(cw_sb[:, :, :], cw_sb[:, :, :],
                             inw_sb[:, 0:2 * D].rearrange("p (a n) -> p a n", a=1).broadcast_to([P, CK, 2 * D]),
                             ALU.mult).then_inc(wz_ready, 1)
            g_.tensor_scalar(th_sb[:, :], th_sb[:, :], float(1 / (2 * np.pi)), 0.0, ALU.mult, ALU.add).then_inc(th_ready, 1)
            steps.then(g_.tensor_tensor(wri_sb[:, :, :, :], wri_sb[:, :, :, :],
                                        ns_sb[:, :, :].rearrange("p r (m a) -> p r m a", a=1).broadcast_to([P, 2, M, H]), ALU.mult))
            for i in range(2 * M):
                g_.tensor_tensor(wbd_sb[:, i, :, :],
                                 wri_sb[:, i // M, i % M, :].rearrange("p (a h) -> p a h", a=1).broadcast_to([P, K, H]),
                                 head_mask[:, :].rearrange("p (k a) -> p k a", a=1).broadcast_to([P, K, H]),
                                 ALU.mult).then_inc(wbd_ready, 1)

            def token_blocks(f):
                pool.wait_ge(slot_ready, f + 1)
                col = lambda ap: ap.rearrange("p (n a) -> p n a", a=1).broadcast_to([P, NT, NBLK])
                g_.tensor_tensor(in_blk[:, :, 0, :], in_blk[:, :, 2, :], col(tile_no[:, :]), ALU.mult).then_inc(in_blk_ready, 1)
                g_.tensor_scalar(in_blk[:, :, 1, :], in_blk[:, :, 2, :], tok_no[:, 0:1], 0.0, ALU.mult, ALU.add).then_inc(in_blk_ready, 1)

            def blocks(f):
                b0 = NBLK * f
                dst = (x1_rows, out)[f]

                def gather(b):
                    g_.indirect_dma_start(out=rows[:, b % RING, :, :].rearrange("p i d -> p (i d)"), out_offset=None, in_=pairs[:, :],
                                          in_offset=bass.IndirectOffsetOnAxis(ap=tok_i[:, b:b + 1], axis=0),
                                          bounds_check=L - 1, oob_is_err=False).then_inc(s_rows[b % RING], 16)

                def scatter(b):
                    pool.wait_ge(yb_ready, b + b0 + 1)
                    g_.indirect_dma_start(out=dst[:, :], out_offset=bass.IndirectOffsetOnAxis(ap=tok_i[:, b:b + 1], axis=0),
                                          in_=res[:, b, :], in_offset=None,
                                          bounds_check=L - 1, oob_is_err=False).then_inc(s_scat, 16)

                pool.wait_ge(tok_ready, f + 1)
                pool.wait_ge(s_pairs, 16 * 2 * NG * (f + 1))
                for b in range(RING):
                    gather(b)
                for b in range(NBLK):
                    scatter(b)
                    if b + RING < NBLK:
                        gather(b + RING)

            def phases(c):
                x_c = val[:, c % 2, :]
                pool.wait_ge(val_ready, c + 1)
                if c >= 1:
                    pool.wait_ge(r_ready, c)
                else:
                    pool.wait_ge(dmix_ready, 1)
                    pool.wait_ge(th_ready, 1)
                for m in range(M - ACT_M[c]):
                    g_.tensor_scalar(ub[:, m, :], x_c, th_sb[:, m:m + 1], 0.0, ALU.mult, ALU.add).then_inc(u_ready, 1)
                if c >= 2:
                    pool.wait_ge(g_ready, c - 1)
                ga_c = ga[:, c % 2, :]
                steps.then(g_.tensor_scalar(ga_c, x_c, dmix[:, 6:7], dmix[:, 4:5], ALU.mult, ALU.add))
                g_.tensor_tensor(ga_c, ga_c, x_c, ALU.mult).then_inc(poly_ready, 1)

            def imag(c):
                pool.wait_ge(g_ready, c + 1)
                pool.wait_ge(sin_ready, c + 1)
                if c >= 1:
                    pool.wait_ge(im_sums, M * c)
                g_.tensor_tensor(imb[:, :, :], sn[:, :, :],
                                 g_sb.rearrange("p (a n) -> p a n", a=1).broadcast_to([P, M, CH]), ALU.mult).then_inc(im_ready, 1)

            def add_squares(c):
                for i, s in enumerate(squares_of(c)):
                    pool.wait_ge(sq_ready, 2 * c + 1 + i)
                    steps.then(g_.tensor_tensor(s[:, 0:2, :], s[:, 0:2, :], s[:, 2:4, :], ALU.add))
                    g_.tensor_tensor(s[:, 0, :], s[:, 0, :], s[:, 1, :], ALU.add).then_inc(sqs_ready, 1)

            token_blocks(0)
            pool.wait_ge(s_b, 32)
            g_.tensor_scalar(b2_sb[:, :, :], b2_sb[:, :, :], 0.5, 0.0, ALU.mult, ALU.add).then_inc(b2_ready, 1)
            blocks(0)
            phases(0)
            phases(1)
            imag(0)
            phases(2)
            imag(1)
            for c in range(NG):
                add_squares(c)
                if c + 3 < NG:
                    phases(c + 3)
                if c + 2 < NG:
                    imag(c + 2)
            token_blocks(1)
            blocks(1)
            pool.wait_ge(s_scat, 16 * 2 * NBLK)

        @block.scalar
        def _(act):
            def normalise(f):
                act.wait_ge(rstd_ready, f + 1)
                if f:
                    act.wait_ge(xt_done, NG)
                    act.wait_ge(s_pairs, 16 * 2 * NG)
                for g in range(NG):
                    for n in range(GT * g + V_TILES[g], GT * (g + 1)):
                        nc.scalar.activation(xn[:, n, :], xr[:, n, :], ACT.Identity, scale=ln[:, 6, n:n + 1],
                                             bias=ln[:, 3, n:n + 1]).then_inc(xna_ready, 1)

            def expand_rs(c):
                act.wait_ge(root_ready, 2 + c + 1)
                if c >= 1:
                    act.wait_ge(rsp_done, c)
                nc.scalar.copy(rs[:, :, :, :].rearrange("p n k h -> p (n k) h"),
                               nw[:, 1, 0:P].rearrange("p (m a) -> p m a", a=1).broadcast_to([P, P, H])).then_inc(rs_ready, 1)

            def normalise_group(g):
                act.wait_ge(rstd_ready, 3 + g)
                act.wait_ge(xt_done, 2 * NG)
                for n in range(GT):
                    nc.scalar.activation(xn[:, GT * g + n, :], xr[:, GT * g + n, :], ACT.Identity, scale=nw[:, 1, P + n:P + n + 1],
                                         bias=ln[:, 3, n:n + 1]).then_inc(xna_ready, 1)

            def to_free(q):
                g = q % NG
                act.wait_ge(xt_done, q + 1)
                nc.scalar.copy(xT[:, PAD + CH * g:PAD + CH * (g + 1)], p_turned(q)[:, :]).then_inc(xT_ready, 1)

            normalise(0)
            to_free(0)
            to_free(1)
            act.wait_ge(pre_dve, 1)
            nc.scalar.activation(ln1[:, 1:2], ln1[:, 0:1], ACT.Exp, scale=-1.0).then_inc(pre_act, 1)
            act.wait_ge(pre_dve, 2)
            nc.scalar.activation(dl_sb[:, :], dl_sb[:, :], ACT.Exp).then_inc(pre_act, 1)
            to_free(2)
            to_free(3)
            act.wait_ge(pre_dve, 3)
            nc.scalar.activation(tw[:, :], pos[:, :], ACT.Exp, scale=ln1[:, 0:1]).then_inc(pre_act, 1)

            def blocks(f):
                b0 = NBLK * f

                def copy_x(b, r):
                    act.wait_ge(tx_done, b + b0 + 1)
                    if isinstance(b, int) and r + b0 >= 2:
                        act.wait_ge(h_done, b + b0 - 1)
                    nc.scalar.copy(xsT[:, r % 2, :], p_xs[r % 2][:, 0:P]).then_inc(xsT_ready, 1)

                def copy_w1(b, r):
                    e = act.value_load(exp_i[0:1, bass.ds(b, 1)], min_val=0, max_val=E - 1)
                    if isinstance(b, int) and r + b0 >= 2:
                        act.wait_ge(h_done, b + b0 - 1)
                    nc.scalar.copy(w1_now[:, r % 2, :], w1_sb[:, bass.ds(e, 1), :].rearrange("p a h -> p (a h)")).then_inc(w1_ready, 1)

                act.wait_ge(tok_ready, f + 1)
                if f == 0:
                    act.wait_ge(s_w1, 16)
                copy_w1(0, 0)
                copy_x(0, 0)
                copy_w1(1, 1)
                copy_x(1, 1)
                for b in range(LEAD):
                    copy_x(b + 2, b + 2)
                    copy_w1(b + 2, b + 2)
                with act.Fori(0, TURNS) as t:
                    for r in range(LEAD, LEAD + RING):
                        copy_x(t * RING + (r + 2), r + 2)
                        copy_w1(t * RING + (r + 2), r + 2)

            def values(c):
                act.wait_ge(zv_done, c + 1)
                if c >= 2:
                    act.wait_ge(poly_ready, c - 1)
                    act.wait_ge(ua_ready, sum(ACT_M[:c - 1]))
                nc.scalar.activation(val[:, c % 2, :], p_a[:, :], ACT.Identity, bias=cbv_sb[:, 0:1]).then_inc(val_ready, 1)

            def score_copy():
                act.wait_ge(s_done, 1)
                nc.scalar.copy(zs[:, 0:PAD], p_y[:, 0:PAD]).then_inc(zs_ready, 1)
                nc.scalar.copy(zs[:, PAD:PAD + CH], p_x[:, :]).then_inc(zs_ready, 1)

            def score_exp():
                act.wait_ge(sx_ready, 1)
                nc.scalar.activation(sx[:, :], sx[:, :], ACT.Exp).then_inc(ex_ready, 1)

            def gates(c):
                act.wait_ge(zg_done, c + 1)
                nc.scalar.activation(gate[:, c, :], p_b[:, :], ACT.Silu, bias=cbv_sb[:, 1:2]).then_inc(gate_ready, 1)

            def phases(c):
                if not ACT_M[c]:
                    return
                act.wait_ge(val_ready, c + 1)
                if c >= 1:
                    act.wait_ge(r_ready, c)
                act.wait_ge(th_ready, 1)
                for m in range(M - ACT_M[c], M):
                    nc.scalar.activation(ub[:, m, :], val[:, c % 2, :], ACT.Identity, scale=th_sb[:, m:m + 1]).then_inc(ua_ready, 1)

            def round_phase(c):
                act.wait_ge(u_ready, M * (c + 1) - sum(ACT_M[:c + 1]))
                act.wait_ge(ua_ready, sum(ACT_M[:c + 1]))
                if c >= 1:
                    act.wait_ge(sin_ready, c)
                nc.scalar.activation(vb[:, :, :], ub[:, :, :], ACT.Identity, bias=round_c[:, :]).then_inc(v_ready, 1)

            def trig(c):
                act.wait_ge(r_ready, c + 1)
                if c >= 2:
                    act.wait_ge(re_sums, M * (c - 1))
                nc.scalar.activation(cs[:, c % 2, :, :], vb[:, :, :], ACT.Abs).then_inc(abs_ready, 1)
                if c >= 1:
                    act.wait_ge(im_ready, c)
                nc.scalar.activation(sn[:, :, :], vb[:, :, :], ACT.Sin, scale=-TWO_PI).then_inc(sin_ready, 1)
                act.wait_ge(abs_ready, c + 1)
                nc.scalar.activation(cs[:, c % 2, :, :], cs[:, c % 2, :, :], ACT.Sin, scale=-TWO_PI, bias=half_pi[:, :]).then_inc(cos_ready, 1)

            def den_squares():
                act.wait_ge(den_ready, 1)
                nc.scalar.activation(den[:, :], den[:, :], ACT.Square, scale=float(np.sqrt(EPS / S_DIV))).then_inc(den2_ready, 1)

            def squares(c):
                if c == NG - 1:
                    act.wait_ge(r_ready, NG)
                    act.wait_ge(sin_ready, NG)
                elif c >= 1:
                    act.wait_ge(sq_done, c)
                re2, im2 = squares_of(c)
                act.wait_ge(re_sums, M * (c + 1))
                nc.scalar.activation(re2[:, :, :], num[:, 0:M, :], ACT.Square).then_inc(sq_ready, 1)
                act.wait_ge(im_sums, M * (c + 1))
                nc.scalar.activation(im2[:, :, :], num[:, M:2 * M, :], ACT.Square).then_inc(sq_ready, 1)

            blocks(0)
            normalise(1)
            to_free(NG)
            to_free(NG + 1)
            values(0)
            score_copy()
            phases(0)
            round_phase(0)
            score_exp()
            values(1)
            gates(0)
            trig(0)
            phases(1)
            round_phase(1)
            den_squares()
            values(2)
            for c in range(NG):
                if c + 1 < NG:
                    trig(c + 1)
                if c + 3 < NG:
                    values(c + 3)
                if c + 2 < NG:
                    phases(c + 2)
                    round_phase(c + 2)
                if c < 2:
                    gates(c + 1)
                squares(c)
                if c == 3:
                    gates(3)
                if c >= 1:
                    expand_rs(c - 1)
                if c in (2, 3):
                    normalise_group(c - 2)
                if c == 2:
                    to_free(2 * NG)
            expand_rs(NG - 1)
            to_free(2 * NG + 1)
            normalise_group(NG - 2)
            to_free(3 * NG - 2)
            blocks(1)

        @block.tensor
        def _(pe):
            mm = nc.tensor.matmul
            pe.wait_ge(const_ready, 1)

            def keep_warm(n):
                ones = ones_b[:, :].rearrange("p (a n) -> p a n", a=1).broadcast_to([P, GT, P])
                for _ in range(n):
                    mm(p_b[:, :], ones_b[:, :], ones, start=True, stop=True)

            def turn(q):
                if 2 * NG < q < 3 * NG - 1:
                    pe.wait_ge(xT_ready, q - 2)
                for n in range(GT):
                    xn_waits(pe, q, n)
                    last = nc.tensor.transpose(p_turned(q)[:, P * n:P * (n + 1)], xn[:, GT * (q % NG) + n, :], ident[:, :])
                last.then_inc(xt_done, 1)

            def xT_wait(q):
                if NG + 2 <= q < 2 * NG or q == 3 * NG - 1:
                    pe.wait_ge(xTv_ready, min(q - NG - 1, 3))
                else:
                    pe.wait_ge(xT_ready, q + 1 if q < 2 * NG else q - 1)

            def logits(q):
                g = q % NG
                xT_wait(q)
                if q >= 2 * NG:
                    pe.wait_ge(val_ready, NG)
                for n in range(GT * g, GT * (g + 1)):
                    last = mm(LOG[:, n, :], xT[:, PAD + P * n:PAD + P * (n + 1)], gw_sb[:, :], start=True, stop=True)
                last.then_inc(lg_done, 1)

            def ranks(f):
                pe.wait_ge(oh_ready, f + 1)
                oh_v = oh[:, :, :].rearrange("p e n -> p (e n)")
                mm(p_m[:, P:2 * P], before[:, :], oh_v, start=True, stop=True)
                mm(p_m[:, 2 * P:3 * P], ones_b[:, :], oh_v, start=True, stop=True).then_inc(rank_done, 1)

            def slot_tokens(f):
                pe.wait_ge(in_blk_ready, 2 * (f + 1))
                pe.wait_ge(in_slot_ready, f + 1)
                for n in range(NT):
                    last = mm(p_c[:, 0:2 * NBLK], in_slot[:, :, n], in_blk[:, n, 0:2, :].rearrange("p i b -> p (i b)"),
                              start=(n == 0), stop=(n == NT - 1))
                last.then_inc(inv_done, 1)

            def blocks(f):
                b0 = NBLK * f

                def turn_x(b, r, t=0):
                    gathers = f * ((NBLK - r % RING + RING - 1) // RING) + r // RING + 1
                    pe.wait_ge(s_rows[r % RING], t * 16 + 16 * gathers)
                    nc.tensor.transpose(p_xs[r % 2][:, 0:P], rows[:, r % RING, 0, :], ident[:, :]).then_inc(tx_done, 1)

                def expert(b):
                    return pe.value_load(exp_i[0:1, bass.ds(b, 1)], min_val=0, max_val=E - 1)

                def hidden(b, r):
                    pe.wait_ge(xsT_ready, b + b0 + 1)
                    pe.wait_ge(w1_ready, b + b0 + 1)
                    for j in range(HC):
                        last = mm(p_h[r % 2][:, P * j:P * (j + 1)], w1_now[:, r % 2, P * j:P * (j + 1)], xsT[:, r % 2, :], start=True, stop=True)
                    last.then_inc(h_done, 1)

                def expert_out(b, r, e):
                    pe.wait_ge(hT_ready, b + b0 + 1)
                    if r + b0 >= 2:
                        pe.wait_ge(yb_ready, b + b0 - 1)
                    for j in range(HC):
                        last = mm(p_ys[r % 2][:, 0:P], hT[:, r % 2, P * j:P * (j + 1)],
                                  w2_sb[:, bass.ds(e, 1), j, :].rearrange("p a d -> p (a d)"),
                                  start=(j == 0), stop=(j == HC - 1))
                    last.then_inc(y_done, 1)

                pe.wait_ge(ids_ready, f + 1)
                turn_x(0, 0)
                turn_x(1, 1)
                hidden(0, 0)
                pe.wait_ge(s_w2, 16)
                for b in range(LEAD):
                    e = expert(b)
                    turn_x(b + 2, b + 2)
                    hidden(b + 1, b + 1)
                    expert_out(b, b, e)
                with pe.Fori(0, TURNS) as t:
                    for r in range(LEAD, LEAD + RING):
                        e = expert(t * RING + r)
                        turn_x(t * RING + (r + 2), r + 2, t)
                        hidden(t * RING + (r + 1), r + 1)
                        expert_out(t * RING + r, r, e)
                for b in range(TAIL, NBLK):
                    if b + 1 < NBLK:
                        hidden(b + 1, b + 1)
                    expert_out(b, b, expert(b))

            def scores():
                for c in range(NG):
                    mm(p_x[K * c:K * (c + 1), :], inw_sb[:, 2 * D:TOTAL], xT[:, PAD + CH * c:PAD + CH * (c + 1)], start=True, stop=True)
                    last = mm(p_y[K * c:K * (c + 1), 0:PAD], inw_sb[:, 2 * D:TOTAL], xT[:, CH * c:CH * c + PAD], start=True, stop=True)
                last.then_inc(s_done, 1)

            def project_values(c):
                if c >= 1:
                    pe.wait_ge(val_ready, c)
                for j in range(CK):
                    last = mm(p_a[:, :], cw_sb[:, j, 0:D], xT[:, CH * c + j:CH * c + j + CH], start=(j == 0), stop=(j == CK - 1))
                last.then_inc(zv_done, 1)

            def project_gates(c):
                if c >= 1:
                    pe.wait_ge(gate_ready, c)
                for j in range(CK):
                    last = mm(p_b[:, :], cw_sb[:, j, D:2 * D], xT[:, CH * c + j:CH * c + j + CH], start=(j == 0), stop=(j == CK - 1))
                last.then_inc(zg_done, 1)

            def spread(dst, src):
                return nc.tensor.transpose(dst, src.rearrange("p k h -> p (k h)"), ident[:, :])

            def weights(c):
                pe.wait_ge(pw_ready, 1)
                if c >= 1:
                    pe.wait_ge(g_ready, c)
                rows_c = slice(K * c, K * (c + 1))
                mm(p_c[:, :], expand[rows_c, :], pw[rows_c, :], start=True, stop=True).then_inc(pwp_done, 1)

            def group_sums():
                pe.wait_ge(sums_ready, 1)
                mm(BEFORE, earlier[:, :], den[:, CH - 1:CH], start=True, stop=True).then_inc(before_done, 1)

            def square_sums(c):
                pe.wait_ge(den2_ready, 1)
                pe.wait_ge(sqs_ready, 2 * (c + 1))
                if c >= 1:
                    pe.wait_ge(rs_ready, c)
                re2, im2 = squares_of(c)
                for n in range(GT):
                    t, rows_c = slice(P * n, P * (n + 1)), slice(K * c, K * (c + 1))
                    mm(SQS[:, K * n:K * (n + 1)], re2[:, 0, t], head_mask[:, :], start=True, stop=False)
                    mm(SQS[:, K * n:K * (n + 1)], im2[:, 0, t], head_mask[:, :], start=False, stop=False)
                    last = mm(SQS[:, K * n:K * (n + 1)], den[rows_c, t], ident[rows_c, rows_c], start=False, stop=True)
                last.then_inc(sq_done, 1)

            def spread_rs(c):
                pe.wait_ge(rs_ready, c + 1)
                if c == NG - 1:
                    pe.wait_ge(g_ready, NG)
                elif c >= 1:
                    pe.wait_ge(x_ready, c)
                for n in range(GT):
                    last = spread(p_rs[c][:, P * n:P * (n + 1)], rs[:, n, :, :])
                last.then_inc(rsp_done, 1)

            def heads(c):
                if c >= 2:
                    pe.wait_ge(yt_ready, c - 1)
                else:
                    pe.wait_ge(zs_ready, 2)
                for i in range(2 * M):
                    if i < M:
                        pe.wait_ge(re_sums, M * c + i + 1)
                    else:
                        if i == M and c >= 1:
                            square_sums(c - 1)
                        pe.wait_ge(im_sums, M * c + i - M + 1)
                    last = mm(p_hd[c % 2][:, :], wbd_sb[:, i, :, :].rearrange("p k h -> p (k h)"), num[:, i, :],
                              start=(i == 0), stop=(i == 2 * M - 1))
                last.then_inc(w_done, 1)

            def outputs(c):
                pe.wait_ge(yt_ready, c + 1)
                if c == NG - 1:
                    pe.wait_ge(x_ready, c)
                for n in range(GT):
                    last = mm(p_d[:, P * n:P * (n + 1)], ygt[:, P * n:P * (n + 1)], ow_sb[:, :], start=True, stop=True)
                last.then_inc(o_done, 1)

            pe.wait_ge(s_x[0], 16)
            keep_warm(18)
            for q in range(NG):
                turn(q)
            pe.wait_ge(s_small, N_SMALL)
            for q in range(NG):
                logits(q)
            ranks(0)
            keep_warm(20)
            slot_tokens(0)
            keep_warm(16)
            blocks(0)
            pe.wait_ge(s_x1[0], 16)
            keep_warm(24)
            turn(NG)
            turn(NG + 1)
            turn(NG + 2)
            turn(NG + 3)
            pe.wait_ge(wz_ready, 1)
            pe.wait_ge(wbd_ready, 2 * M)
            xT_wait(NG)
            project_values(0)
            xT_wait(NG + 1)
            xT_wait(2 * NG - 1)
            scores()
            project_values(1)
            project_gates(0)
            weights(0)
            project_values(2)
            group_sums()
            weights(1)
            project_gates(1)
            project_values(3)
            for c in range(NG - 1):
                heads(c)
                if c == NG - 2:
                    project_gates(NG - 1)
                if c >= 1:
                    spread_rs(c - 1)
                if c + 2 < NG:
                    weights(c + 2)
                if c == 2:
                    turn(2 * NG)
                if c >= 1:
                    outputs(c - 1)
                if c == 0:
                    project_gates(2)
            heads(NG - 1)
            pe.wait_ge(gate_ready, NG)
            keep_warm(8)
            spread_rs(NG - 2)
            square_sums(NG - 1)
            keep_warm(4)
            outputs(NG - 2)
            logits(2 * NG)
            turn(2 * NG + 1)
            keep_warm(5)
            spread_rs(NG - 1)
            keep_warm(2)
            outputs(NG - 1)
            logits(2 * NG + 1)
            keep_warm(22)
            turn(3 * NG - 2)
            turn(3 * NG - 1)
            logits(3 * NG - 2)
            logits(3 * NG - 1)
            ranks(1)
            keep_warm(17)
            slot_tokens(1)
            keep_warm(20)
            blocks(1)

        @block.vector
        def _(dve):
            steps, roots = Steps(dve, dve_step), Steps(dve, root_ready)
            v = nc.vector
            ts, tt, stt = v.tensor_scalar, v.tensor_tensor, v.scalar_tensor_tensor

            def over(ap, n):
                return ap.rearrange("p (a m) -> p a m", a=1).broadcast_to([ap.shape[0], n, ap.shape[1]])

            def each(ap, n):
                return ap.rearrange("p (m a) -> p m a", a=1).broadcast_to([ap.shape[0], ap.shape[1], n])

            def rsqrt(y, a, t):
                steps.then(ts(y.bitcast(I32), a.bitcast(I32), -0.5, RSQRT_SEED, ALU.mult, ALU.add))
                for i in range(3):
                    steps.then(stt(t, y, -0.5, y, ALU.mult, ALU.mult))
                    steps.then(tt(t, t, a, ALU.mult))
                    (roots if i == 2 else steps).then(stt(y, t, 1.5, y, ALU.add, ALU.mult))

            def row_stats(n0, nt, loads=None):
                for n in range(n0, n0 + nt):
                    if loads and n % GT == 0:
                        dve.wait_ge(loads[n // GT], 16)
                    steps.did(v.bn_stats(st[:, n, :], xr[:, n, :]))

            def moments(n0, nt, var):
                tiles, at = slice(0, nt), slice(n0, n0 + nt)
                steps.wait()
                steps.did(tt(ln[:, 0, tiles], st[:, at, 1], st[:, at, 4], ALU.subtract))
                steps.did(tt(ln[:, 1, tiles], st[:, at, 1], st[:, at, 4], ALU.add))
                steps.then(tt(ln[:, 2, tiles], st[:, at, 2], st[:, at, 5], ALU.add))
                steps.did(stt(ln[:, 3, tiles], ln[:, 0, tiles], 0.25, ln[:, 0, tiles], ALU.mult, ALU.mult))
                steps.did(ts(ln[:, 4, tiles], ln[:, 1, tiles], 0.5, None, ALU.mult))
                steps.then(ts(ln[:, 2, tiles], ln[:, 2, tiles], 1.0 / D, EPS, ALU.mult, ALU.add))
                steps.then(tt(var, ln[:, 2, tiles], ln[:, 3, tiles], ALU.add))

            def normalise(q, n0, rstd, ahead=0):
                tiles = range(V_TILES[q % NG] if q < 2 * NG else GT)
                for n in tiles:
                    ts(xn[:, n0 + n, :], xr[:, n0 + n, :], ln[:, 4, ahead + n:ahead + n + 1], rstd[:, ahead + n:ahead + n + 1],
                       ALU.subtract, ALU.mult).then_inc(xn_ready, 1)

            def norm(f):
                row_stats(0, NT, (s_x, s_x1)[f])
                moments(0, NT, ln[:, 5, :])
                rsqrt(ln[:, 6, :], ln[:, 5, :], ln[:, 7, :])
                stt(ln[:, 3, :], ln[:, 4, :], -1.0, ln[:, 6, :], ALU.mult, ALU.mult).then_inc(rstd_ready, 1)
                if f:
                    dve.wait_ge(xt_done, NG)
                    dve.wait_ge(s_pairs, 16 * 2 * NG)
                for g in range(NG):
                    normalise(NG * f + g, GT * g, ln[:, 6, :], GT * g)

            def route(f):
                dve.wait_ge(lg_done, NG * (f + 1))
                by_token = lg[:, :, :].rearrange("p e n -> p n e")
                steps.then(tt(by_token, LOG, over(gb_sb[:, :], NT), ALU.add))
                steps.then(v.tensor_reduce(mx[:, :], by_token, AX.X, ALU.max))
                steps.then(tt(rt[:, 0, :, :], lg[:, :, :], over(mx[:, :], E), ALU.is_equal))
                steps.then(tt(rt[:, 0, :, :], rt[:, 0, :, :], each(rev_e[:, :], NT), ALU.mult))
                steps.then(v.tensor_reduce(mx[:, :], rt[:, 0, :, :].rearrange("p e n -> p n e"), AX.X, ALU.max))
                tt(oh[:, :, :], rt[:, 0, :, :], over(mx[:, :], E), ALU.is_equal).then_inc(oh_ready, 1)
                dve.wait_ge(rank_done, f + 1)
                steps.then(v.tensor_tensor_scan(rt[:, 1, :, :].rearrange("p e n -> p (e n)"),
                                                first_tile[:, :, :].rearrange("p e n -> p (e n)"),
                                                p_m[:, 2 * P:3 * P], 0.0, ALU.mult, ALU.add))
                steps.did(tt(rt[:, 0, :, :], rt[:, 1, :, :], TOT, ALU.subtract))
                steps.then(ts(re8[:, 0, :], rt[:, 1, :, NT - 1], 1.0 / P, 0.5 - 1.0 / (2 * P), ALU.mult, ALU.add))
                steps.did(tt(rt[:, 0, :, :], rt[:, 0, :, :], RANK, ALU.add))
                steps.then(ts(re8[:, 0, :], re8[:, 0, :], ROUND_POS, ROUND_POS, ALU.add, ALU.subtract))
                steps.then(v.tensor_tensor_scan(re8[:, 1, :], ones_e[:, :], re8[:, 0, :], 0.0, ALU.mult, ALU.add))
                steps.then(tt(re8[:, 2, :], re8[:, 1, :], re8[:, 0, :], ALU.subtract))
                steps.then(stt(rt[:, 0, :, :], each(re8[:, 2, :], NT), float(P), rt[:, 0, :, :], ALU.mult, ALU.add))
                steps.then(tt(rt[:, 0, :, :], rt[:, 0, :, :], oh[:, :, :], ALU.mult))
                steps.then(v.tensor_reduce(mx[:, :], rt[:, 0, :, :].rearrange("p e n -> p n e"), AX.X, ALU.add))
                steps.then(ts(slot_b[:, :], mx[:, :], 1.0 / P, 1.0 / (2 * P) - 0.5, ALU.mult, ALU.add))
                steps.then(ts(slot_b[:, :], slot_b[:, :], ROUND, ROUND, ALU.add, ALU.subtract))
                tt(in_blk[:, :, 2, :], each(slot_b[:, :], NBLK), over(blk_no[:, :], NT), ALU.is_equal).then_inc(slot_ready, 1)
                steps.then(stt(slot_s[:, :], slot_b[:, :], -float(P), mx[:, :], ALU.mult, ALU.add))
                if f == 0:
                    dve.wait_ge(wbd_ready, 2 * M)
                tt(in_slot, over(slot_s[:, :], P), slot_no[:, :, :], ALU.is_equal).then_inc(in_slot_ready, 1)
                steps.then(tt(cmp_b[:, :, :], each(blk_no[0:1, :], E), over(re8[0:1, 1, :], NBLK), ALU.is_ge))
                steps.then(v.tensor_reduce(exp_f[:, :], cmp_b[:, :, :], AX.X, ALU.add))
                ts(exp_i[:, :], exp_f[:, :], float(E - 1), None, ALU.min).then_inc(ids_ready, 1)
                dve.wait_ge(inv_done, f + 1)
                steps.then(stt(inv[:, 0, :], INV[:, 0, :], 0.0, no_tok[:, :], ALU.is_equal, ALU.mult))
                steps.then(stt(inv[:, 0, :], INV[:, 0, :], float(P), inv[:, 0, :], ALU.mult, ALU.add))
                stt(tok_i[:, :], inv[:, 0, :], -float(P), INV[:, 1, :], ALU.add, ALU.add).then_inc(tok_ready, 1)
                dve.wait_ge(ids_ready, f + 1)
                dve.wait_ge(tok_ready, f + 1)

            def blocks(f):
                b0 = NBLK * f

                def relu(b, r):
                    e = dve.value_load(exp_i[0:1, bass.ds(b, 1)], min_val=0, max_val=E - 1)
                    dve.wait_ge(h_done, b + b0 + 1)
                    if isinstance(b, int) and r + b0 >= 2:
                        dve.wait_ge(y_done, b + b0 - 1)
                    for j in range(HC):
                        last = ts(hT[:, r % 2, P * j:P * (j + 1)], p_h[r % 2][:, P * j:P * (j + 1)],
                                  b1_sb[:, bass.ds(e, 1), j], 0.0, ALU.add, ALU.max)
                    last.then_inc(hT_ready, 1)
                    return e

                def add_x(b, r, e):
                    tt(rows[:, r % RING, 1, :], rows[:, r % RING, 1, :],
                       b2_sb[:, bass.ds(e, 1), :].rearrange("p a d -> p (a d)"), ALU.add).then_inc(xb_ready, 1)

                def sums(b, r):
                    dve.wait_ge(y_done, b + b0 + 1)
                    dve.wait_ge(xb_ready, b + b0 + 1)
                    stt(res[:, bass.ds(b, 1), :].rearrange("p a d -> p (a d)"), p_ys[r % 2][:, 0:P], 0.5,
                        rows[:, r % RING, 1, :], ALU.mult, ALU.add).then_inc(yb_ready, 1)

                if f == 0:
                    dve.wait_ge(s_b, 32)
                    dve.wait_ge(b2_ready, 1)
                add_x(0, 0, relu(0, 0))
                for b in range(LEAD):
                    add_x(b + 1, b + 1, relu(b + 1, b + 1))
                    sums(b, b)
                with dve.Fori(0, TURNS) as t:
                    for r in range(LEAD, LEAD + RING):
                        e = relu(t * RING + (r + 1), r + 1)
                        add_x(t * RING + (r + 1), r + 1, e)
                        sums(t * RING + r, r)
                for b in range(TAIL, NBLK):
                    if b + 1 < NBLK:
                        add_x(b + 1, b + 1, relu(b + 1, b + 1))
                    sums(b, b)

            def prelude():
                dve.wait_ge(s_small, N_SMALL)
                dve.wait_ge(pos_ready, NG)
                slope = sp_sb[:, CK + 2:CK + 3]
                ts(ln1[:, 0:1].bitcast(I32), slope.bitcast(I32), 0x7FFFFFFF, None, ALU.bitwise_and).then_inc(pre_dve, 1)
                steps.then(v.tensor_reduce(dmix[:, 0:1], dl_sb[:, :], AX.X, ALU.max))
                ts(dl_sb[:, :], dl_sb[:, :], dmix[:, 0:1], None, ALU.subtract).then_inc(pre_dve, 1)
                steps.then(ts(head_i[:, :], head_i[:, :], K - 1, None, ALU.bitwise_and))
                steps.then(ts(anchor[:, 0:1], head_i[:, :], float(K - A), None, ALU.is_ge))
                steps.did(ts(anchor[:, 1:2], anchor[:, 0:1], 2.0, -1.0, ALU.mult, ALU.add))
                steps.then(ts(anchor[:, 2:3], anchor[:, 0:1], -float(L - 1), float(L - 1), ALU.mult, ALU.add))
                steps.did(ts(pos[:, :], pos[:, :], anchor[:, 1:2], anchor[:, 2:3], ALU.mult, ALU.add))
                dve.wait_ge(pre_act, 1)
                steps.then(ts(ln1[:, 2:3], ln1[:, 1:2], 2.0, None, ALU.add))
                steps.then(v.reciprocal(ln1[:, 2:3], ln1[:, 2:3]))
                steps.then(tt(ln1[:, 1:2], ln1[:, 1:2], ln1[:, 2:3], ALU.mult))
                steps.then(tt(ln1[:, 2:3], ln1[:, 1:2], ln1[:, 1:2], ALU.mult))
                steps.then(ts(ln1[:, 3:4], ln1[:, 2:3], 1.0 / 15, None, ALU.mult))
                for n in range(13, 1, -2):
                    steps.then(stt(ln1[:, 3:4], ln1[:, 3:4], 1.0 / n, ln1[:, 2:3], ALU.add, ALU.mult))
                steps.then(stt(ln1[:, 3:4], ln1[:, 3:4], 1.0, ln1[:, 1:2], ALU.add, ALU.mult))
                steps.then(ts(ln1[:, 4:5], slope, 0.0, None, ALU.max))
                stt(ln1[:, 0:1], ln1[:, 3:4], -2.0, ln1[:, 4:5], ALU.mult, ALU.subtract).then_inc(pre_dve, 1)
                dve.wait_ge(pre_act, 2)
                steps.then(v.tensor_reduce(dmix[:, 1:2], dl_sb[:, :], AX.X, ALU.add))
                steps.then(v.reciprocal(dmix[:, 2:3], dmix[:, 1:2]))
                steps.then(ts(dmix[:, 3:6], dl_sb[:, :], dmix[:, 2:3], None, ALU.mult))
                ts(dmix[:, 6:7], dmix[:, 5:6], -1.0, None, ALU.mult).then_inc(dmix_ready, 1)
                dve.wait_ge(dmix_ready, 1)

            def score_weights():
                tap = lambda j: sp_sb[:, j:j + 1]
                dve.wait_ge(zs_ready, 2)
                steps.then(ts(sx[:, :], zs[:, PAD:PAD + CH], tap(CK - 1), sp_sb[:, CK:CK + 1], ALU.mult, ALU.add))
                for j in range(CK - 1):
                    steps.then(stt(sx[:, :], zs[:, j:j + CH], tap(j), sx[:, :], ALU.mult, ALU.add))
                steps.then(ts(sx[:, :], sx[:, :], sp_sb[:, CK + 1:CK + 2], -20.0, ALU.mult, ALU.max))
                ts(sx[:, :], sx[:, :], 20.0, None, ALU.min).then_inc(sx_ready, 1)

            def time_weights():
                dve.wait_ge(ex_ready, 1)
                dve.wait_ge(pre_act, 3)
                tt(pw[:, :], sx[:, :], tw[:, :], ALU.mult).then_inc(pw_ready, 1)

            def reduce_phase(c):
                dve.wait_ge(v_ready, c + 1)
                stt(vb[:, :, :], vb[:, :, :], ROUND, ub[:, :, :], ALU.subtract, ALU.subtract).then_inc(r_ready, 1)

            def envelope(c):
                dve.wait_ge(poly_ready, c + 1)
                dve.wait_ge(pwp_done, c + 1)
                if c >= 1:
                    dve.wait_ge(im_ready, c)
                stt(g_sb, ga[:, c % 2, :], dmix[:, 3:4], p_c[:, :], ALU.add, ALU.mult).then_inc(g_ready, 1)

            def den_sums():
                v.tensor_tensor_scan(den[:, :], pw[:, :], pw[:, :], 0.0, ALU.add, ALU.bypass).then_inc(sums_ready, 1)
                dve.wait_ge(before_done, 1)
                ts(den[:, :], den[:, :], BEFORE, 1e-4, ALU.add, ALU.max).then_inc(den_ready, 1)

            def real(c):
                dve.wait_ge(cos_ready, c + 1)
                dve.wait_ge(g_ready, c + 1)
                tt(cs[:, c % 2, :, :], cs[:, c % 2, :, :], over(g_sb, M), ALU.mult).then_inc(re_ready, 1)

            def running_sums(c):
                dve.wait_ge(re_ready, c + 1)
                if c >= 1:
                    dve.wait_ge(sq_ready, 2 * c)
                    dve.wait_ge(w_done, c)
                for m in range(M):
                    v.tensor_tensor_scan(num[:, m, :], cs[:, c % 2, m, :], cs[:, c % 2, m, :], carry[:, m, :], ALU.add, ALU.bypass).then_inc(re_sums, 1)
                dve.wait_ge(im_ready, c + 1)
                for m in range(M):
                    v.tensor_tensor_scan(num[:, M + m, :], imb[:, m, :], imb[:, m, :], carry[:, M + m, :], ALU.add, ALU.bypass).then_inc(im_sums, 1)
                dve.wait_ge(re_sums, M * (c + 1))
                dve.wait_ge(im_sums, M * (c + 1))
                steps.then(v.tensor_copy(carry[:, 0:2 * M, :], num[:, 0:2 * M, CH - 1:CH]))

            def attend(c):
                dve.wait_ge(o_done, c + 1)
                t = slice(GT * c, GT * (c + 1))
                tt(xr[:, t, :], xr[:, t, :], p_d[:, :].rearrange("p (n d) -> p n d", d=D), ALU.add).then_inc(x_ready, 1)

            def group_stats(c):
                dve.wait_ge(x_ready, c + 1)
                row_stats(GT * c, GT)

            def tail(c_rs, c_ln):
                if c_ln is not None:
                    moments(GT * c_ln, GT, nw[:, 0, P:P + GT])
                dve.wait_ge(sq_done, c_rs + 1)
                steps.then(ts(nw[:, 0, 0:P], SQS, S_DIV, None, ALU.mult))
                used = slice(0, P if c_ln is None else P + GT)
                if c_rs:
                    dve.wait_ge(rs_ready, c_rs)
                rsqrt(nw[:, 1, used], nw[:, 0, used], nw[:, 2, used])
                if c_ln is not None:
                    stt(ln[:, 3, 0:GT], ln[:, 4, 0:GT], -1.0, nw[:, 1, P:P + GT], ALU.mult, ALU.mult).then_inc(rstd_ready, 1)

            def norm_last():
                dve.wait_ge(xna_ready, 2 * (NT - sum(V_TILES)) + GT * (NG - 2))
                pair = slice(P, P + 2 * GT)
                moments(NT - 2 * GT, 2 * GT, nw[:, 0, pair])
                rsqrt(nw[:, 1, pair], nw[:, 0, pair], nw[:, 2, pair])
                stt(ln[:, 3, 0:GT], ln[:, 4, 0:GT], -1.0, nw[:, 1, P:P + GT], ALU.mult, ALU.mult).then_inc(rstd_ready, 1)
                dve.wait_ge(xt_done, 2 * NG)
                normalise(3 * NG - 1, NT - GT, nw[:, 1, pair], GT)
                dve.wait_ge(xt_done, 3 * NG)
                v.tensor_copy(xT[:, PAD + L - CH:PAD + L], p_turned(3 * NG - 1)[:, :]).then_inc(xTv_ready, 1)

            def gate_heads(c):
                dve.wait_ge(w_done, c + 1)
                dve.wait_ge(gate_ready, c + 1)
                if c >= 1:
                    dve.wait_ge(o_done, c)
                steps.then(tt(ygt, gate[:, c, :], p_hd[c % 2][:, :], ALU.mult))

            def scale_heads(c):
                dve.wait_ge(rsp_done, c + 1)
                tt(ygt, ygt, p_rs[c][:, :], ALU.mult).then_inc(yt_ready, 1)

            norm(0)
            prelude()
            route(0)
            blocks(0)
            norm(1)
            for g in (2, 3):
                dve.wait_ge(xt_done, NG + g + 1)
                v.tensor_copy(xT[:, PAD + CH * g:PAD + CH * (g + 1)], p_turned(NG + g)[:, :]).then_inc(xTv_ready, 1)
            score_weights()
            reduce_phase(0)
            time_weights()
            envelope(0)
            den_sums()
            real(0)
            reduce_phase(1)
            for c in range(NG):
                running_sums(c)
                if c + 1 < NG:
                    envelope(c + 1)
                    real(c + 1)
                if c >= 2:
                    attend(c - 2)
                    group_stats(c - 2)
                if c >= 1:
                    tail(c - 1, c - 2 if c >= 2 else None)
                if c + 2 < NG:
                    reduce_phase(c + 2)
                if c >= 1:
                    gate_heads(c - 1)
                    scale_heads(c - 1)
            tail(NG - 1, None)
            gate_heads(NG - 1)
            attend(NG - 2)
            scale_heads(NG - 1)
            group_stats(NG - 2)
            attend(NG - 1)
            group_stats(NG - 1)
            norm_last()
            route(1)
            blocks(1)


def kernel(**inputs):
    import concourse.bacc as _bacc
    from concourse.bass_utils import run_bass_kernel_spmd as _run

    a = {k.removeprefix("L0_"): np.asarray(v) for k, v in inputs.items()}
    wri = np.stack([a["attn_W_re"].reshape(H, M, H), a["attn_W_im"].reshape(H, M, H)], axis=1)
    slopes = np.concatenate([a["attn_decay_slopes"], a["attn_anchor_slopes"]])
    ns = a["attn_norm_scale"].reshape(2, H, M).transpose(1, 0, 2)
    heads = np.concatenate([a["attn_conv_w"].reshape(CK, TOTAL)[:, 2 * D:], a["attn_conv_b"][None, 2 * D:],
                            a["attn_score_scale"][None], slopes[None]]).T
    arrays = {
        "x": a["attn_x"].reshape(L, D),
        "gate_w": a["ffn_gate_w"].T,
        "gate_b": a["ffn_gate_b"].reshape(1, E),
        "w1": a["ffn_w1"].transpose(2, 0, 1),
        "b1": a["ffn_b1"].reshape(E, HC, P).transpose(2, 0, 1),
        "w2": a["ffn_w2"].reshape(E, D, HC, P).transpose(3, 0, 2, 1),
        "b2": a["ffn_b2"].reshape(1, E * D),
        "in_w": a["attn_in_proj_w"],
        "conv_w": a["attn_conv_w"].reshape(CK, TOTAL)[:, :2 * D].reshape(1, CK * 2 * D),
        "conv_b": a["attn_conv_b"].reshape(1, TOTAL),
        "theta": a["attn_theta"].reshape(K * H, M),
        "score_par": np.broadcast_to(heads, (NG, K, CK + 3)).reshape(P, CK + 3),
        "deriv": a["attn_deriv_logits"].reshape(1, 3),
        "norm_scale": np.broadcast_to(ns, (K, H, 2, M)).reshape(P, 2, M),
        "w_reim": np.broadcast_to(wri, (K, H, 2, M, H)).reshape(P, 2, M, H),
        "out_w": a["attn_out_proj_w"],
    }
    arrays = {k: np.ascontiguousarray(v) for k, v in arrays.items()}
    nc = _bacc.Bacc("TRN2", target_bir_lowering=False, num_devices=1)
    args = [nc.dram_tensor(f"in_{k}", v.shape, mybir.dt.from_np(v.dtype), kind="ExternalInput").ap()
            for k, v in arrays.items()]
    out = nc.dram_tensor("out_x", (L, D), F32, kind="ExternalOutput").ap()
    build(nc, *args, out)
    r = _run(nc, [{f"in_{k}": v for k, v in arrays.items()}], core_ids=[0])
    return r.results[0]["out_x"].reshape(1, L, D)
```
